# Optimizing a Trainium2 kernel written in Bass

```python
import numpy as np
import jax
import jax.numpy as jnp

def _softmax(x, axis=-1):
    return jax.nn.softmax(x, axis=axis)

def _gelu(x):
    return jax.nn.gelu(x, approximate=True)

def _silu(x):
    return jax.nn.silu(x)

def _sigmoid(x):
    return jax.nn.sigmoid(x)

def _layernorm(x, axis=-1, eps=1e-05):
    m = jnp.mean(x, axis=axis, keepdims=True)
    v = jnp.var(x, axis=axis, keepdims=True)
    return (x - m) / jnp.sqrt(v + eps)

def _scatter_add(tgt, idx, src, axis=0):
    return tgt.at[idx].add(src)

def _segment_sum(src, seg, n):
    return jax.ops.segment_sum(src, seg, n)
kernel_name = 'mk_dlrm_tower_d1_rec_r8_0e01f6'

def setup_inputs(seed: int=0):
    np.random.seed(seed)
    _w = jnp.asarray

    def _rec_inputs():
        import jax
        import jax.numpy as jnp
        _tk = jax.random.key(seed)
        dense_ctx = jax.random.normal(jax.random.fold_in(_tk, 190), (512, 16), jnp.float32)
        ids = jnp.stack([jax.random.randint(jax.random.fold_in(_tk, 200 + f), (512,), 0, v, jnp.int32) for f, v in enumerate([12500, 125000, 125000, 1000, 1250, 12500, 1000, 1250, 125000, 1000, 1250, 1250, 1000, 12500, 12500, 1250, 1000, 1000, 1250, 1000, 12500, 12500, 1000, 12500, 1250, 12500, 1250, 1250, 1000, 1000, 1000, 1000])], axis=1)
        tbl_0 = 0.05 * jax.random.normal(jax.random.fold_in(_tk, 500 + 0), (12500, 64), jnp.float32)
        tbl_1 = 0.05 * jax.random.normal(jax.random.fold_in(_tk, 500 + 1), (125000, 64), jnp.float32)
        tbl_2 = 0.05 * jax.random.normal(jax.random.fold_in(_tk, 500 + 2), (125000, 64), jnp.float32)
        tbl_3 = 0.05 * jax.random.normal(jax.random.fold_in(_tk, 500 + 3), (1000, 64), jnp.float32)
        tbl_4 = 0.05 * jax.random.normal(jax.random.fold_in(_tk, 500 + 4), (1250, 64), jnp.float32)
        tbl_5 = 0.05 * jax.random.normal(jax.random.fold_in(_tk, 500 + 5), (12500, 64), jnp.float32)
        tbl_6 = 0.05 * jax.random.normal(jax.random.fold_in(_tk, 500 + 6), (1000, 64), jnp.float32)
        tbl_7 = 0.05 * jax.random.normal(jax.random.fold_in(_tk, 500 + 7), (1250, 64), jnp.float32)
        tbl_8 = 0.05 * jax.random.normal(jax.random.fold_in(_tk, 500 + 8), (125000, 64), jnp.float32)
        tbl_9 = 0.05 * jax.random.normal(jax.random.fold_in(_tk, 500 + 9), (1000, 64), jnp.float32)
        tbl_10 = 0.05 * jax.random.normal(jax.random.fold_in(_tk, 500 + 10), (1250, 64), jnp.float32)
        tbl_11 = 0.05 * jax.random.normal(jax.random.fold_in(_tk, 500 + 11), (1250, 64), jnp.float32)
        tbl_12 = 0.05 * jax.random.normal(jax.random.fold_in(_tk, 500 + 12), (1000, 64), jnp.float32)
        tbl_13 = 0.05 * jax.random.normal(jax.random.fold_in(_tk, 500 + 13), (12500, 64), jnp.float32)
        tbl_14 = 0.05 * jax.random.normal(jax.random.fold_in(_tk, 500 + 14), (12500, 64), jnp.float32)
        tbl_15 = 0.05 * jax.random.normal(jax.random.fold_in(_tk, 500 + 15), (1250, 64), jnp.float32)
        tbl_16 = 0.05 * jax.random.normal(jax.random.fold_in(_tk, 500 + 16), (1000, 64), jnp.float32)
        tbl_17 = 0.05 * jax.random.normal(jax.random.fold_in(_tk, 500 + 17), (1000, 64), jnp.float32)
        tbl_18 = 0.05 * jax.random.normal(jax.random.fold_in(_tk, 500 + 18), (1250, 64), jnp.float32)
        tbl_19 = 0.05 * jax.random.normal(jax.random.fold_in(_tk, 500 + 19), (1000, 64), jnp.float32)
        tbl_20 = 0.05 * jax.random.normal(jax.random.fold_in(_tk, 500 + 20), (12500, 64), jnp.float32)
        tbl_21 = 0.05 * jax.random.normal(jax.random.fold_in(_tk, 500 + 21), (12500, 64), jnp.float32)
        tbl_22 = 0.05 * jax.random.normal(jax.random.fold_in(_tk, 500 + 22), (1000, 64), jnp.float32)
        tbl_23 = 0.05 * jax.random.normal(jax.random.fold_in(_tk, 500 + 23), (12500, 64), jnp.float32)
        tbl_24 = 0.05 * jax.random.normal(jax.random.fold_in(_tk, 500 + 24), (1250, 64), jnp.float32)
        tbl_25 = 0.05 * jax.random.normal(jax.random.fold_in(_tk, 500 + 25), (12500, 64), jnp.float32)
        tbl_26 = 0.05 * jax.random.normal(jax.random.fold_in(_tk, 500 + 26), (1250, 64), jnp.float32)
        tbl_27 = 0.05 * jax.random.normal(jax.random.fold_in(_tk, 500 + 27), (1250, 64), jnp.float32)
        tbl_28 = 0.05 * jax.random.normal(jax.random.fold_in(_tk, 500 + 28), (1000, 64), jnp.float32)
        tbl_29 = 0.05 * jax.random.normal(jax.random.fold_in(_tk, 500 + 29), (1000, 64), jnp.float32)
        tbl_30 = 0.05 * jax.random.normal(jax.random.fold_in(_tk, 500 + 30), (1000, 64), jnp.float32)
        tbl_31 = 0.05 * jax.random.normal(jax.random.fold_in(_tk, 500 + 31), (1000, 64), jnp.float32)
        _rk = jax.random.fold_in(_tk, 7)
        W_top1 = 0.0606339 * jax.random.normal(jax.random.fold_in(_tk, 801), (272, 512), jnp.float32)
        W_top2 = 0.0441942 * jax.random.normal(jax.random.fold_in(_tk, 802), (512, 256), jnp.float32)
        W_top3 = 0.0625 * jax.random.normal(jax.random.fold_in(_tk, 803), (256, 1), jnp.float32)
        b_top1 = jnp.zeros((512,), jnp.float32)
        b_top2 = jnp.zeros((256,), jnp.float32)
        return (dense_ctx, ids, tbl_0, tbl_1, tbl_2, tbl_3, tbl_4, tbl_5, tbl_6, tbl_7, tbl_8, tbl_9, tbl_10, tbl_11, tbl_12, tbl_13, tbl_14, tbl_15, tbl_16, tbl_17, tbl_18, tbl_19, tbl_20, tbl_21, tbl_22, tbl_23, tbl_24, tbl_25, tbl_26, tbl_27, tbl_28, tbl_29, tbl_30, tbl_31, W_top1, b_top1, W_top2, b_top2, W_top3)
    dense_ctx, ids, tbl_0, tbl_1, tbl_2, tbl_3, tbl_4, tbl_5, tbl_6, tbl_7, tbl_8, tbl_9, tbl_10, tbl_11, tbl_12, tbl_13, tbl_14, tbl_15, tbl_16, tbl_17, tbl_18, tbl_19, tbl_20, tbl_21, tbl_22, tbl_23, tbl_24, tbl_25, tbl_26, tbl_27, tbl_28, tbl_29, tbl_30, tbl_31, W_top1, b_top1, W_top2, b_top2, W_top3 = _rec_inputs()

    def _L0_rec_setup():
        import jax, jax.numpy as jnp
        import numpy as np
        EMB_DIM = 64
        NUM_FIELDS = 32
        NUM_PAIRS = NUM_FIELDS * (NUM_FIELDS - 1) // 2
        D1 = 256
        BATCH = 256
        key = jax.random.key(seed)
        k1, k2, k3 = jax.random.split(key, 3)
        feat_emb = jax.random.normal(k1, (BATCH, NUM_FIELDS, EMB_DIM), dtype=jnp.float32)
        lim_k = float(np.sqrt(6.0 / (EMB_DIM + EMB_DIM)))
        kernel = jax.random.uniform(k2, (EMB_DIM, NUM_PAIRS, EMB_DIM), minval=-lim_k, maxval=lim_k, dtype=jnp.float32)
        lim_w = float(np.sqrt(6.0 / (NUM_PAIRS + D1)))
        W = jax.random.uniform(k3, (D1, NUM_PAIRS), minval=-lim_w, maxval=lim_w, dtype=jnp.float32)
        b = jnp.zeros((D1,), dtype=jnp.float32)
        return {'feat_emb': feat_emb, 'kernel': kernel, 'W': W, 'b': b}
    _L0_rec_all = _L0_rec_setup()
    _L0_rec_in = {k: v for k, v in _L0_rec_all.items() if k in ('kernel', 'W', 'b')}
    del _L0_rec_all
    return {'dense_ctx': dense_ctx, 'ids': ids, 'tbl_0': tbl_0, 'tbl_1': tbl_1, 'tbl_2': tbl_2, 'tbl_3': tbl_3, 'tbl_4': tbl_4, 'tbl_5': tbl_5, 'tbl_6': tbl_6, 'tbl_7': tbl_7, 'tbl_8': tbl_8, 'tbl_9': tbl_9, 'tbl_10': tbl_10, 'tbl_11': tbl_11, 'tbl_12': tbl_12, 'tbl_13': tbl_13, 'tbl_14': tbl_14, 'tbl_15': tbl_15, 'tbl_16': tbl_16, 'tbl_17': tbl_17, 'tbl_18': tbl_18, 'tbl_19': tbl_19, 'tbl_20': tbl_20, 'tbl_21': tbl_21, 'tbl_22': tbl_22, 'tbl_23': tbl_23, 'tbl_24': tbl_24, 'tbl_25': tbl_25, 'tbl_26': tbl_26, 'tbl_27': tbl_27, 'tbl_28': tbl_28, 'tbl_29': tbl_29, 'tbl_30': tbl_30, 'tbl_31': tbl_31, 'W_top1': W_top1, 'b_top1': b_top1, 'W_top2': W_top2, 'b_top2': b_top2, 'W_top3': W_top3, 'L0_rec_kernel': _L0_rec_in['kernel'], 'L0_rec_W': _L0_rec_in['W'], 'L0_rec_b': _L0_rec_in['b']}

def reference(dense_ctx, ids, tbl_0, tbl_1, tbl_2, tbl_3, tbl_4, tbl_5, tbl_6, tbl_7, tbl_8, tbl_9, tbl_10, tbl_11, tbl_12, tbl_13, tbl_14, tbl_15, tbl_16, tbl_17, tbl_18, tbl_19, tbl_20, tbl_21, tbl_22, tbl_23, tbl_24, tbl_25, tbl_26, tbl_27, tbl_28, tbl_29, tbl_30, tbl_31, W_top1, b_top1, W_top2, b_top2, W_top3, L0_rec_kernel, L0_rec_W, L0_rec_b):
    import jax
    import jax.numpy as jnp

    def _L0_rec_ref(feat_emb, kernel, W, b):
        import jax, jax.numpy as jnp
        import numpy as np
        EMB_DIM = 64
        NUM_FIELDS = 32
        NUM_PAIRS = NUM_FIELDS * (NUM_FIELDS - 1) // 2
        D1 = 256
        BATCH = 256
        num_fields = feat_emb.shape[1]
        rows, cols = np.triu_indices(num_fields, k=1)
        p = feat_emb[:, rows, :]
        q = feat_emb[:, cols, :]
        pij = jnp.einsum('bpe,dpe,bpd->bp', p, kernel, q)
        return pij @ W.T + b
    e = jnp.stack([tbl_0[ids[:, 0]], tbl_1[ids[:, 1]], tbl_2[ids[:, 2]], tbl_3[ids[:, 3]], tbl_4[ids[:, 4]], tbl_5[ids[:, 5]], tbl_6[ids[:, 6]], tbl_7[ids[:, 7]], tbl_8[ids[:, 8]], tbl_9[ids[:, 9]], tbl_10[ids[:, 10]], tbl_11[ids[:, 11]], tbl_12[ids[:, 12]], tbl_13[ids[:, 13]], tbl_14[ids[:, 14]], tbl_15[ids[:, 15]], tbl_16[ids[:, 16]], tbl_17[ids[:, 17]], tbl_18[ids[:, 18]], tbl_19[ids[:, 19]], tbl_20[ids[:, 20]], tbl_21[ids[:, 21]], tbl_22[ids[:, 22]], tbl_23[ids[:, 23]], tbl_24[ids[:, 24]], tbl_25[ids[:, 25]], tbl_26[ids[:, 26]], tbl_27[ids[:, 27]], tbl_28[ids[:, 28]], tbl_29[ids[:, 29]], tbl_30[ids[:, 30]], tbl_31[ids[:, 31]]], axis=1)
    z = _L0_rec_ref(e, L0_rec_kernel, L0_rec_W, L0_rec_b)
    z = z.reshape(z.shape[0], -1)
    h = jnp.concatenate([z, dense_ctx], axis=1)
    h = jnp.maximum(h @ W_top1 + b_top1, 0.0)
    h = jnp.maximum(h @ W_top2 + b_top2, 0.0)
    y = h @ W_top3
    return y

_drawn_inputs = setup_inputs


def setup_inputs(seed=0):
    import zlib

    import numpy as np

    out = dict(_drawn_inputs(seed))
    spreads = {'b_top1': (0.0, 0.1), 'b_top2': (0.0, 0.1), 'L0_rec_b': (0.0, 0.1)}
    factors = {'tbl_0': 3.323,
     'tbl_1': 3.261,
     'tbl_2': 3.251,
     'tbl_3': 3.278,
     'tbl_4': 3.591,
     'tbl_5': 3.531,
     'tbl_6': 3.114,
     'tbl_7': 3.0,
     'tbl_8': 3.402,
     'tbl_9': 2.95,
     'tbl_10': 3.255,
     'tbl_11': 3.066,
     'tbl_12': 3.089,
     'tbl_13': 3.438,
     'tbl_14': 3.139,
     'tbl_15': 3.264,
     'tbl_16': 3.603,
     'tbl_17': 2.984,
     'tbl_18': 3.488,
     'tbl_19': 3.094,
     'tbl_20': 3.143,
     'tbl_21': 3.391,
     'tbl_22': 3.672,
     'tbl_23': 3.029,
     'tbl_24': 3.25,
     'tbl_25': 2.934,
     'tbl_26': 3.119,
     'tbl_27': 3.564,
     'tbl_28': 3.693,
     'tbl_29': 3.362,
     'tbl_30': 3.389,
     'tbl_31': 3.233}
    for name, (base, spread) in spreads.items():
        noise = np.random.default_rng([zlib.crc32(name.encode()), seed]).standard_normal(out[name].shape)
        drawn = base * np.exp(spread * noise) if base else spread * noise
        out[name] = jnp.asarray(drawn.astype(out[name].dtype))
    for name, factor in factors.items():
        out[name] = (out[name] * factor).astype(out[name].dtype)
    return out
```

```python
from contextlib import ExitStack

import concourse.bass as bass
from concourse import mybir

BATCH, FIELDS, DIM, DENSE = 512, 32, 64, 16
PAIRS = FIELDS * (FIELDS - 1) // 2
P = 128
BT = BATCH // P
QUAD = 4
QUADS = FIELDS // QUAD
Z_OUT, H1, H2 = 256, 512, 256

PIECES = [(q, r) for q in range(QUADS) for r in range(q + 1)]
FULL, SINGLE = 0, 1


def groups_of(q, r):
    if r < q:
        return [[(FULL, [(k, 0), (k, 1)]), (FULL, [(k, 2), (k, 3)])] for k in (2 * r, 2 * r + 1)]
    return [[(FULL, [(2 * r, 2), (2 * r, 3)]), (SINGLE, [(2 * r, 1), (2 * r + 1, 3)])]]


GROUPS = [(n, q, r, g) for n, (q, r) in enumerate(PIECES) for g in groups_of(q, r)]
GROUPS_BEFORE_QUAD = [sum(1 for _, q, _, _ in GROUPS if q < m) for m in range(QUADS + 1)]
GROUPS_TO_PIECE = [sum(1 for p, *_ in GROUPS if p <= n) for n in range(len(PIECES))]
LAST_UNIT = {(q, c): k for _, q, _, g in GROUPS for _, units in g for k, c in units}

RAW, SPLIT, AHEAD = 3, 3, 2
PRODUCTS = 4
T_BUFS = 2
SETUP_TILES = 5
QUAD_TILES = QUAD + QUAD // 2
LATE = [6]
SPREAD = [1, 1, 1, 1, 1, 1]
FIRST_SPREAD_QUAD = 4


def pair_index(i, j):
    return i * FIELDS - i * (i + 1) // 2 + j - i - 1


def spread(q):
    return SPREAD if q >= FIRST_SPREAD_QUAD else LATE


def tiles_after():
    out = {}
    for q in range(QUADS - 1):
        tiles = [(q + 1, t) for t in range(QUAD_TILES)]
        counts = spread(q)
        for back, count in enumerate(counts):
            g = GROUPS_BEFORE_QUAD[q + 1] - len(counts) + back
            out[g], tiles = tiles[:count], tiles[count:]
    return out


def build(nc, dense, ids, tables, w1, b1, w2, b2, w3, kern, w, b, out):
    F32, F32R, I32, U32 = mybir.dt.float32, mybir.dt.float32r, mybir.dt.int32, mybir.dt.uint32
    ALU, ACT = mybir.AluOpType, mybir.ActivationFunctionType
    TILES_AFTER = tiles_after()
    prepared_in = {}
    for q in range(QUADS - 1):
        first = GROUPS[GROUPS_BEFORE_QUAD[q + 1] - len(spread(q))][0]
        prepared_in[first] = q + 1

    with ExitStack() as ctx:
        def sb(name, shape, dt=F32):
            return ctx.enter_context(nc.sbuf_tensor(name, shape, dt))

        def sem(name):
            return ctx.enter_context(nc.semaphore(name))

        ids_sb = sb("ids_sb", [P, BT, FIELDS], I32)
        nat = sb("nat", [P, FIELDS // 2, BT, 2, DIM])
        parts = sb("parts", [P, 2, QUAD * BT, 2, DIM], F32R)
        moving = sb("moving", [P, 2, QUAD, BATCH], F32R)
        factor = sb("factor", [P, FIELDS // 2, BATCH])
        k_raw = sb("k_raw", [P, RAW, QUAD, QUAD * DIM])
        k_high = sb("k_high", [P, SPLIT, 2, QUAD, 2 * DIM], F32R)
        k_low = sb("k_low", [P, SPLIT, 2, QUAD, 2 * DIM], F32R)
        prod = sb("prod", [P, PRODUCTS, 2, BATCH])
        prod1 = sb("prod1", [P, 2, BATCH])
        select = sb("select", [P, 62])
        ident = sb("ident", [P, P])
        pij = sb("pij", [P, QUADS, BATCH])
        w_sb = sb("w_sb", [P, 2, PAIRS])
        w_slots = sb("w_slots", [P, 2, FIELDS, FIELDS])
        w_t = sb("w_t", [P, QUADS, Z_OUT])
        w1_sb = sb("w1_sb", [P, 2, H1])
        w1d_sb = sb("w1d_sb", [DENSE, H1])
        w2_sb = sb("w2_sb", [P, 4, H2])
        w3_sb = sb("w3_sb", [P, 2])
        b_sb = sb("b_sb", [P, 2])
        b1_sb = sb("b1_sb", [P, 4])
        b2_sb = sb("b2_sb", [P, 2])
        dense_sb = sb("dense_sb", [P, BT, DENSE])
        dense_t = sb("dense_t", [DENSE, BATCH])
        tail = nat[:].rearrange("p f t h e -> p f (t h e)")
        z_sb, h1_sb, h2_sb = tail[:, 0:2, :], tail[:, 2:6, :], tail[:, 6:8, :]
        y_sb = sb("y_sb", [1, BATCH])

        t_ps = ctx.enter_context(nc.psum_tensor("t_ps", [P, T_BUFS, 2, BATCH], F32))
        tr_ps = ctx.enter_context(nc.psum_tensor("tr_ps", [P, 2, BATCH], F32))
        sum_ps = ctx.enter_context(nc.psum_tensor("sum_ps", [P, 2, BATCH], F32))

        ids_loaded = sem("ids_loaded")
        w_loaded = sem("w_loaded")
        small_loaded = sem("small_loaded")
        gathered = [sem(f"gathered{q}") for q in range(QUADS)]
        k_loaded = [sem(f"k_loaded{s}") for s in range(RAW)]
        ident_ready = sem("ident_ready")
        zeroed = sem("zeroed")
        zeroed_dve = sem("zeroed_dve")
        slots_ready = sem("slots_ready")
        high_ready = sem("high_ready")
        parts_ready = sem("parts_ready")
        transposed = sem("transposed")
        tile_copied = sem("tile_copied")
        k_high_ready = sem("k_high_ready")
        k_split = sem("k_split")
        t_ready = sem("t_ready")
        multiplied = sem("multiplied")
        reduced = sem("reduced")
        pij_copied = sem("pij_copied")
        z_ready = sem("z_ready")
        z_copied = sem("z_copied")
        z_copied_dve = sem("z_copied_dve")
        h1_ready = sem("h1_ready")
        h1_even = sem("h1_even")
        h1_odd = sem("h1_odd")
        h2_ready = sem("h2_ready")
        h2_even = sem("h2_even")
        h2_odd = sem("h2_odd")
        y_ready = sem("y_ready")
        y_copied = sem("y_copied")
        stored = sem("stored")

        def loads_of(q, r):
            for h in range(2):
                i = 4 * r + 2 * h
                c = 0 if r < q else 2 * h + 1
                at = pair_index(i, QUAD * q + c)
                yield 2 * h, c, QUAD - c, bass.AP(
                    kern.tensor, at * DIM,
                    [[PAIRS * DIM, DIM], [(FIELDS - 2 - i) * DIM, 2], [1, (QUAD - c) * DIM]])

        def nat_of(q):
            return nat[:, 2 * q:2 * q + 2, :, :, :].rearrange("p f t h e -> p (f t h) e")

        def k_views(n, row, c):
            raw = k_raw[:, n % RAW, row:row + 2, c * DIM:].rearrange("p r (c e) -> p r c e", e=DIM)
            return raw, *(x[:, n % SPLIT, row // 2, c:, :].rearrange("p c (r e) -> p r c e", r=2) for x in (k_high, k_low))

        block = ctx.enter_context(nc.Block())


        @block.sync
        def _(sp):
            sp.dma_start(ids_sb[:], ids.rearrange("(t p) f -> p t f", p=P)).then_inc(ids_loaded, 16)
            for n, (q, r) in enumerate(PIECES):
                if n >= RAW:
                    sp.wait_ge(k_split, n - RAW + 1)
                for row, c, _, view in loads_of(q, r):
                    for half in range(2):
                        sp.dma_start(k_raw[DIM * half:DIM * half + DIM, n % RAW, row:row + 2, c * DIM:],
                                     view).then_inc(k_loaded[n % RAW], 16)
            sp.wait_ge(y_copied, 1)
            sp.dma_start(out.rearrange("b o -> o b"), y_sb[:]).then_inc(stored, 16)
            sp.wait_ge(stored, 16)

        @block.gpsimd
        def _(pool):
            nc.gpsimd.memset(ident[:], 0.0).then_inc(zeroed, 1)
            pool.wait_ge(zeroed, 1)
            nc.gpsimd.affine_select(out=ident[:], in_=ident[:], compare_op=ALU.not_equal, fill=1.0, base=0,
                                    pattern=[[-1, P]], channel_multiplier=1).then_inc(ident_ready, 1)
            pool.wait_ge(ids_loaded, 16)
            for f in range(FIELDS):
                for t in range(BT):
                    nc.gpsimd.indirect_dma_start(
                        nat[:, f // 2, t, f % 2, :], None, tables[f],
                        bass.IndirectOffsetOnAxis(ap=ids_sb[:, t, f:f + 1].bitcast(U32), axis=0),
                    ).then_inc(gathered[f // QUAD], 16)

        @block.scalar
        def _(act):
            act.dma_start(w_sb[:], w.rearrange("(p c) n -> p c n", p=P)).then_inc(w_loaded, 16)
            small = [(dense_sb, dense.rearrange("(t p) n -> p t n", p=P)),
                     (w1_sb, w1[0:Z_OUT, :].rearrange("(p c) n -> p c n", p=P)),
                     (w1d_sb, w1[Z_OUT:Z_OUT + DENSE, :]),
                     (w2_sb, w2.rearrange("(p c) n -> p c n", p=P)),
                     (w3_sb, w3.rearrange("(p c) o -> p (c o)", p=P)),
                     (b_sb, b.rearrange("(p c) -> p c", p=P)),
                     (b1_sb, b1.rearrange("(p c) -> p c", p=P)),
                     (b2_sb, b2.rearrange("(p c) -> p c", p=P))]
            for to, of in small:
                act.dma_start(to[:], of).then_inc(small_loaded, 16)

            def split_high(n):
                q, r = PIECES[n]
                act.wait_ge(k_loaded[n % RAW], 64 * (n // RAW + 1))
                if n >= SPLIT:
                    act.wait_ge(t_ready, 2 * GROUPS_TO_PIECE[n - SPLIT])
                for row, c, _, _ in loads_of(q, r):
                    raw, high, _ = k_views(n, row, c)
                    last = nc.scalar.copy(high, raw)
                last.then_inc(k_high_ready, 1)

            def copy_tile(q, t):
                n = SETUP_TILES + QUAD_TILES * q + t
                act.wait_ge(transposed, n + 1)
                if t < QUAD:
                    if q >= 2:
                        act.wait_ge(t_ready, 2 * GROUPS_BEFORE_QUAD[q - 1])
                    to = moving[:, q % 2, t, :]
                else:
                    to = factor[:, 2 * q + t - QUAD, :]
                nc.scalar.copy(to, tr_ps[:, n % 2, :]).then_inc(tile_copied, 1)

            def high_parts(q):
                act.wait_ge(gathered[q], 16 * QUAD * BT)
                if q >= 2:
                    act.wait_ge(transposed, SETUP_TILES + QUAD_TILES * (q - 1))
                nc.scalar.copy(parts[:, q % 2, :, 0, :],
                               nat_of(q)).then_inc(high_ready, 1)

            def copy_sums(q):
                act.wait_ge(reduced, GROUPS_BEFORE_QUAD[q + 1])
                if q == 0:
                    for c in range(1, QUAD):
                        last = nc.scalar.copy(pij[32 * c:32 * c + 32, 0, :], sum_ps[32 * c:32 * c + 32, 0, :])
                else:
                    last = nc.scalar.copy(pij[:, q, :], sum_ps[:, q % 2, :])
                last.then_inc(pij_copied, 1)

            for n in range(AHEAD):
                split_high(n)
            for n in range(SETUP_TILES):
                act.wait_ge(transposed, n + 1)
                if n < SETUP_TILES - 1:
                    to, of = w_t[:, 2 * n:2 * n + 2, :].rearrange("p q o -> p (q o)"), tr_ps[:, n % 2, :]
                else:
                    to, of = dense_t[:], tr_ps[0:DENSE, n % 2, :]
                nc.scalar.copy(to, of).then_inc(tile_copied, 1)
            high_parts(0)
            for t in range(QUAD_TILES):
                copy_tile(0, t)
            for n, (q, r) in enumerate(PIECES):
                if n + AHEAD < len(PIECES):
                    split_high(n + AHEAD)
                if r == 0 and q:
                    copy_sums(q - 1)
                if n in prepared_in:
                    high_parts(prepared_in[n])
                for g, (piece, *_) in enumerate(GROUPS):
                    if piece == n:
                        for tile in TILES_AFTER.get(g, []):
                            copy_tile(*tile)
            copy_sums(QUADS - 1)

            act.wait_ge(small_loaded, 16 * len(small))
            act.wait_ge(z_ready, 1)
            nc.scalar.activation(z_sb[:, 0, :], tr_ps[:, 0, :], ACT.Identity, bias=b_sb[:, 0:1]).then_inc(z_copied, 1)
            for n in (0, 2):
                act.wait_ge(h1_ready, n + 1)
                nc.scalar.activation(h1_sb[:, n, :], t_ps[:, n // 2, n % 2, :], ACT.Relu,
                                     bias=b1_sb[:, n:n + 1]).then_inc(h1_even, 1)
            act.wait_ge(h2_ready, 1)
            nc.scalar.activation(h2_sb[:, 0, :], sum_ps[:, 0, :], ACT.Relu, bias=b2_sb[:, 0:1]).then_inc(h2_even, 1)
            act.wait_ge(y_ready, 1)
            nc.scalar.copy(y_sb[:], tr_ps[0:1, 0, :]).then_inc(y_copied, 1)

        @block.vector
        def _(dve):
            def split_low(n):
                q, r = PIECES[n]
                dve.wait_ge(k_high_ready, n + 1)
                for row, c, _, _ in loads_of(q, r):
                    raw, high, low = k_views(n, row, c)
                    last = nc.vector.tensor_tensor(low, raw, high, ALU.subtract)
                last.then_inc(k_split, 1)

            def low_parts(q):
                dve.wait_ge(high_ready, q + 1)
                nc.vector.tensor_tensor(parts[:, q % 2, :, 1, :],
                                        nat_of(q),
                                        parts[:, q % 2, :, 0, :], ALU.subtract).then_inc(parts_ready, 1)

            def multiply(g, half):
                _, q, r, batches = GROUPS[g]
                kind, units = batches[half]
                n = 2 * g + half
                k = units[0][0]
                dve.wait_ge(t_ready, n + 1)
                if half == 0 or kind == SINGLE:
                    dve.wait_ge(tile_copied, SETUP_TILES + QUAD_TILES * (r + 1))
                if kind == FULL:
                    if n >= PRODUCTS:
                        dve.wait_ge(reduced, n // 2 - PRODUCTS // 2 + 1)
                    nc.vector.tensor_tensor(prod[:, n % PRODUCTS, :, :], t_ps[:, n % T_BUFS, :, :],
                                            factor[:, k:k + 1, :].broadcast_to([P, 2, BATCH]),
                                            ALU.mult).then_inc(multiplied, 1)
                else:
                    if q:
                        dve.wait_ge(reduced, GROUPS_BEFORE_QUAD[q])
                    nc.vector.tensor_tensor(prod1[0:DIM, :, :], t_ps[0:DIM, n % T_BUFS, :, :],
                                            factor[0:DIM, k:k + 2, :], ALU.mult).then_inc(multiplied, 1)

            nc.vector.memset(select[:], 0.0)
            nc.vector.memset(w_slots[:], 0.0).then_inc(zeroed_dve, 1)
            dve.wait_ge(zeroed_dve, 1)
            nc.vector.memset(select[0:DIM, 30:31], 1.0)
            nc.vector.memset(select[DIM:P, 31:32], 1.0)
            nc.vector.memset(pij[0:32, 0, :], 0.0)
            nc.vector.memset(prod1[DIM:P, :, :], 0.0)
            dve.wait_ge(w_loaded, 16)
            for i in range(FIELDS - 1):
                at = pair_index(i, i + 1)
                last = nc.vector.tensor_copy(w_slots[:, :, i + 1:, i], w_sb[:, :, at:at + FIELDS - 1 - i])
            last.then_inc(slots_ready, 1)
            for n in range(AHEAD):
                split_low(n)
            low_parts(0)
            g = 0
            for n, (q, r) in enumerate(PIECES):
                late = n in prepared_in and prepared_in[n] - 1 < FIRST_SPREAD_QUAD
                if n in prepared_in and not late:
                    low_parts(prepared_in[n])
                if n + AHEAD < len(PIECES):
                    split_low(n + AHEAD)
                for _ in groups_of(q, r):
                    multiply(g, 0)
                    multiply(g, 1)
                    g += 1
                if late:
                    low_parts(prepared_in[n])

            dve.wait_ge(small_loaded, 16 * len(range(8)))
            dve.wait_ge(z_ready, 2)
            nc.vector.tensor_scalar(z_sb[:, 1, :], tr_ps[:, 1, :], b_sb[:, 1:2], None, ALU.add).then_inc(z_copied_dve, 1)
            for n in (1, 3):
                dve.wait_ge(h1_ready, n + 1)
                nc.vector.tensor_scalar(h1_sb[:, n, :], t_ps[:, n // 2, n % 2, :], b1_sb[:, n:n + 1], 0.0,
                                        ALU.add, ALU.max).then_inc(h1_odd, 1)
            dve.wait_ge(h2_ready, 2)
            nc.vector.tensor_scalar(h2_sb[:, 1, :], sum_ps[:, 1, :], b2_sb[:, 1:2], 0.0,
                                    ALU.add, ALU.max).then_inc(h2_odd, 1)

        @block.tensor
        def _(pe):
            def free_tile(n):
                if n >= 2:
                    pe.wait_ge(tile_copied, n - 1)

            def transpose_tile(q, t):
                n = SETUP_TILES + QUAD_TILES * q + t
                if t == 0:
                    pe.wait_ge(parts_ready, q + 1)
                free_tile(n)
                for s in range(BT):
                    if t < QUAD:
                        of = parts[:, q % 2, (t // 2 * BT + s) * 2 + t % 2, :, :].bitcast(F32)
                    else:
                        of = nat[:, 2 * q + t - QUAD, s, :, :]
                    of = of.rearrange("p h e -> p (h e)")
                    last = nc.tensor.transpose(tr_ps[:, n % 2, P * s:P * s + P], of, ident[:])
                last.then_inc(transposed, 1)

            def contract(g):
                n, q, r, batches = GROUPS[g]
                first_of_piece = g == 0 or GROUPS[g - 1][0] != n
                if first_of_piece:
                    pe.wait_ge(k_split, n + 1)
                    pe.wait_ge(tile_copied, SETUP_TILES + QUAD_TILES * q + QUAD)
                for half, (_, units) in enumerate(batches):
                    batch = 2 * g + half
                    if batch >= T_BUFS:
                        pe.wait_ge(multiplied, batch - T_BUFS + 1)
                    for u, (k, c) in enumerate(units):
                        for which, part in enumerate((k_high, k_low)):
                            last = nc.tensor.matmul(t_ps[:, batch % T_BUFS, u, :],
                                                    part[:, n % SPLIT, k - 2 * r, c, :],
                                                    moving[:, q % 2, c, :],
                                                    start=which == 0, stop=which == 1)
                    last.then_inc(t_ready, 1)

            def reduce(g):
                _, q, r, batches = GROUPS[g]
                if g == GROUPS_BEFORE_QUAD[q] and q >= 2:
                    pe.wait_ge(pij_copied, q - 1)
                pe.wait_ge(multiplied, 2 * g + 2)
                for half, (kind, units) in enumerate(batches):
                    for u, (k, c) in enumerate(units):
                        of = prod[:, (2 * g + half) % PRODUCTS, u, :] if kind == FULL else prod1[:, u, :]
                        last = nc.tensor.matmul(sum_ps[32 * c:32 * c + 32, q % 2, :],
                                                select[:, 30 - 2 * k:62 - 2 * k], of,
                                                start=k == 0, stop=k == LAST_UNIT[q, c])
                last.then_inc(reduced, 1)

            pe.wait_ge(ident_ready, 1)
            pe.wait_ge(slots_ready, 1)
            for n in range(SETUP_TILES - 1):
                free_tile(n)
                for s in range(4):
                    q, c = 2 * n + s // 2, s % 2
                    last = nc.tensor.transpose(
                        tr_ps[:, n % 2, P * s:P * s + P],
                        w_slots[:, c, QUAD * q:QUAD * q + QUAD, :].rearrange("p j i -> p (j i)"), ident[:])
                last.then_inc(transposed, 1)
            free_tile(SETUP_TILES - 1)
            pe.wait_ge(small_loaded, 16 * 8)
            for s in range(BT):
                last = nc.tensor.transpose(tr_ps[0:DENSE, (SETUP_TILES - 1) % 2, P * s:P * s + P], dense_sb[:, s, :], ident[:])
            last.then_inc(transposed, 1)

            for t in range(QUAD_TILES):
                transpose_tile(0, t)
            for g in range(len(GROUPS)):
                contract(g)
                if g:
                    reduce(g - 1)
                for q, t in TILES_AFTER.get(g, []):
                    transpose_tile(q, t)

            pe.wait_ge(tile_copied, SETUP_TILES + QUAD_TILES * QUADS)
            pe.wait_ge(pij_copied, QUADS - 1)
            for c in range(2):
                for q in range(QUADS - 1):
                    nc.tensor.matmul(tr_ps[:, c, :], w_t[:, q, P * c:P * c + P], pij[:, q, :],
                                     start=q == 0, stop=False)
            reduce(len(GROUPS) - 1)
            pe.wait_ge(pij_copied, QUADS)
            q = QUADS - 1
            for c in range(2):
                nc.tensor.matmul(tr_ps[:, c, :], w_t[:, q, P * c:P * c + P], pij[:, q, :],
                                 start=False, stop=True).then_inc(z_ready, 1)
            for n in range(4):
                nc.tensor.matmul(t_ps[:, n // 2, n % 2, :], w1d_sb[:, n::4], dense_t[:], start=True, stop=False)
            pe.wait_ge(z_copied, 1)
            pe.wait_ge(z_copied_dve, 1)
            for n in range(4):
                for c in range(2):
                    last = nc.tensor.matmul(t_ps[:, n // 2, n % 2, :], w1_sb[:, c, n::4], z_sb[:, c, :],
                                            start=False, stop=c == 1)
                last.then_inc(h1_ready, 1)
            for c in range(4):
                pe.wait_ge(h1_odd if c % 2 else h1_even, c // 2 + 1)
                for n in range(2):
                    last = nc.tensor.matmul(sum_ps[:, n, :], w2_sb[:, c, n::2], h1_sb[:, c, :],
                                            start=c == 0, stop=c == 3)
                    if c == 3:
                        last.then_inc(h2_ready, 1)
            for c in range(2):
                pe.wait_ge(h2_odd if c else h2_even, 1)
                last = nc.tensor.matmul(tr_ps[0:1, 0, :], w3_sb[:, c:c + 1], h2_sb[:, c, :], start=c == 0, stop=c == 1)
            last.then_inc(y_ready, 1)


_TABLES = [f"tbl_{f}" for f in range(FIELDS)]
_INS = ["dense_ctx", "ids"] + _TABLES + ["W_top1", "b_top1", "W_top2", "b_top2", "W_top3",
                                          "L0_rec_kernel", "L0_rec_W", "L0_rec_b"]


def kernel(**inputs):
    import numpy as _np
    import concourse.bacc as _bacc
    from concourse import mybir as _mybir
    from concourse.bass_utils import run_bass_kernel_spmd as _run

    nc = _bacc.Bacc("TRN2", target_bir_lowering=False, num_devices=1)
    arrays, args = {}, {}
    for name in _INS:
        a = _np.ascontiguousarray(inputs[name])
        arrays[f"in_{name}"] = a
        args[name] = nc.dram_tensor(f"in_{name}", a.shape, _mybir.dt.from_np(a.dtype), kind="ExternalInput").ap()
    out = nc.dram_tensor("out_y", (BATCH, 1), _mybir.dt.float32, kind="ExternalOutput").ap()
    build(nc, args["dense_ctx"], args["ids"], [args[t] for t in _TABLES], args["W_top1"], args["b_top1"],
          args["W_top2"], args["b_top2"], args["W_top3"], args["L0_rec_kernel"], args["L0_rec_W"],
          args["L0_rec_b"], out)
    r = _run(nc, [arrays], core_ids=[0])
    return r.results[0]["out_y"]
```

```python
from contextlib import ExitStack

import concourse.bass as bass
from concourse import mybir

BATCH, FIELDS, DIM, DENSE = 512, 32, 64, 16
PAIRS = FIELDS * (FIELDS - 1) // 2
P = 128
BT = BATCH // P
QUAD = 4
QUADS = FIELDS // QUAD
Z_OUT, H1, H2 = 256, 512, 256

PIECES = [(q, r) for q in range(QUADS) for r in range(q + 1)]
FULL, SINGLE = 0, 1


def groups_of(q, r):
    if r < q:
        return [[(FULL, [(k, 0), (k, 1)]), (FULL, [(k, 2), (k, 3)])] for k in (2 * r, 2 * r + 1)]
    return [[(FULL, [(2 * r, 2), (2 * r, 3)]), (SINGLE, [(2 * r, 1), (2 * r + 1, 3)])]]


GROUPS = [(n, q, r, g) for n, (q, r) in enumerate(PIECES) for g in groups_of(q, r)]
GROUPS_BEFORE_QUAD = [sum(1 for _, q, _, _ in GROUPS if q < m) for m in range(QUADS + 1)]
GROUPS_TO_PIECE = [sum(1 for p, *_ in GROUPS if p <= n) for n in range(len(PIECES))]
LAST_UNIT = {(q, c): k for _, q, _, g in GROUPS for _, units in g for k, c in units}

RAW, SPLIT, AHEAD = 3, 3, 2
POOL_FROM = 18
PAIRED = False
PRODUCTS = 6
T_BUFS = 3
NAT_QUADS = 4

CHUNKS = 5
CHUNK = [2, 1, 0, 4, 0, 1, 2, 3]
FIRST_ROW = [28, 24, 20, 0, 0, 0, 0, 0]
ADDED = (4, 5, 6)

W_ROWS = 3
W_FROM = 54
PICKED = (3, 6, 7)
GATHERED = [f for f in range(FIELDS) if f not in PICKED]
LATE_FIELDS = (11,)
ONE_HOTS = 4
CUTS_MAX = 10

FIRST_TILES = [("ids", 0)] + [("index", f) for f in PICKED]
FIRST_TILES += [("moving", 3), ("moving", 0), ("moving", 6), ("moving", 1), ("factor", 0), ("moving", 2),
                ("factor", 1), ("moving", 7), ("factor", 3), ("moving", 4)]
TILES_AFTER = {0: [("moving", 5), ("factor", 2)],
               1: [("moving", 8)],
               2: [("moving", 9), ("factor", 4)],
               3: [("moving", 10), ("moving", 11), ("factor", 5)],
               5: [("moving", 12)],
               6: [("moving", 13)],
               7: [("factor", 6), ("moving", 14)],
               8: [("moving", 15), ("factor", 7)]}
for _q in range(3, QUADS - 1):
    _f = QUAD * (_q + 1)
    _tiles = [("moving", _f), ("moving", _f + 1), ("factor", _f // 2),
              ("moving", _f + 2), ("moving", _f + 3), ("factor", _f // 2 + 1)]
    _groups = range(GROUPS_BEFORE_QUAD[_q], GROUPS_BEFORE_QUAD[_q + 1])[-len(_tiles):]
    for _n, _tile in enumerate(_tiles):
        TILES_AFTER.setdefault(_groups[_n * len(_groups) // len(_tiles)], []).append(_tile)
for _n, _tile in enumerate([("w", n) for n in range((2 * CHUNKS + 3) // 4)] + [("dense", 0)]):
    TILES_AFTER.setdefault(W_FROM + _n, []).append(_tile)
TILES = FIRST_TILES + [tile for g in range(len(GROUPS)) for tile in TILES_AFTER.get(g, [])]
TILE = {tile: n for n, tile in enumerate(TILES)}
FIELDS_DONE = [max(TILE["moving", f] for f in range(QUAD * q, QUAD * q + QUAD)) + 1 for q in range(QUADS)]


def fields_after(g):
    return [x for n in (g, g + 1) for kind, x in TILES_AFTER.get(n, []) if kind == "moving" and (x in LATE_FIELDS) == (n == g)]


def in_t_ps(n):
    return n % 2 == 1 and n < FIELDS_DONE[1]


def pair_index(i, j):
    return i * FIELDS - i * (i + 1) // 2 + j - i - 1


def reductions_after(g):
    q = max(m for m in range(QUADS) if GROUPS_BEFORE_QUAD[m] <= g)
    if not g:
        return ()
    if g == GROUPS_BEFORE_QUAD[q]:
        return (g - 1,) if (g - 1 - GROUPS_BEFORE_QUAD[q - 1]) % 2 == 0 or not PAIRED else (g - 2, g - 1)
    if not PAIRED:
        return (g - 1,)
    return (g - 2, g - 1) if (g - GROUPS_BEFORE_QUAD[q]) % 2 == 0 else ()


def build(nc, dense, ids, tables, w1, b1, w2, b2, w3, kern, w, b, out):
    F32, F32R, I32, U32 = mybir.dt.float32, mybir.dt.float32r, mybir.dt.int32, mybir.dt.uint32
    ALU, ACT = mybir.AluOpType, mybir.ActivationFunctionType
    with ExitStack() as ctx:
        def sb(name, shape, dt=F32):
            return ctx.enter_context(nc.sbuf_tensor(name, shape, dt))

        def sem(name):
            return ctx.enter_context(nc.semaphore(name))

        ids_sb = sb("ids_sb", [P, BT, FIELDS], I32)
        nat = sb("nat", [P, NAT_QUADS * 2, BT, 2, DIM])
        parts = sb("parts", [P, 2 * QUAD, BT, 2, DIM], F32R)
        moving = sb("moving", [P, 2, QUAD, BATCH], F32R)
        factor = sb("factor", [P, FIELDS // 2, BATCH])
        k_raw = sb("k_raw", [P, RAW, QUAD, QUAD * DIM])
        k_high = sb("k_high", [P, SPLIT, 2, QUAD, 2 * DIM], F32R)
        k_low = sb("k_low", [P, SPLIT, 2, QUAD, 2 * DIM], F32R)
        prod = sb("prod", [P, PRODUCTS, 2, BATCH])
        prod1 = sb("prod1", [P, 2, BATCH])
        SMALL = 8
        select = sb("select", [P, 62])
        ident = sb("ident", [P, P])
        pij = sb("pij", [P, CHUNKS, BATCH])
        w_sb = sb("w_sb", [P, 2, PAIRS])
        w_t = sb("w_t", [P, CHUNKS * Z_OUT])
        w_slots = sb("w_slots", [P, 2, CHUNKS, QUAD, FIELDS])
        prod_flat = prod[:].rearrange("p n h b -> p (n h b)")
        cuts = {f: next(c for c in range(1, CUTS_MAX + 1) if tables[f].shape[0] % c == 0 and tables[f].shape[0] // c <= P)
                for f in PICKED}
        rows_of = {f: tables[f].shape[0] // cuts[f] for f in PICKED}
        at = len(PICKED) * BATCH
        index = prod_flat[:, 2 * BATCH:2 * BATCH + at].rearrange("p (n b) -> p n b", b=BATCH)
        at += 2 * BATCH
        table_raw = prod_flat[:, at:at + len(PICKED) * CUTS_MAX * DIM].rearrange("p (n c e) -> p n c e", n=len(PICKED), e=DIM)
        table_parts = sb("table_parts", [P, 2, CUTS_MAX, 2, DIM], F32R)
        one_hot_ring = sb("one_hot_ring", [P, ONE_HOTS, BATCH], F32R)
        one_hot = [one_hot_ring[:, n, :] for n in range(ONE_HOTS)]
        ids_f = sb("ids_f", [P, BT, FIELDS])
        ids_t = sb("ids_t", [FIELDS, BATCH], F32R)
        row_pick = sb("row_pick", [FIELDS, len(PICKED), P], F32R)
        first_row = sb("first_row", [P, len(PICKED)])
        first_row_i = sb("first_row_i", [P, len(PICKED)], I32)
        add_halves = sb("add_halves", [P, 3 * DIM], F32R)
        late_sums = sb("late_sums", [P, BATCH])
        w1_sb = sb("w1_sb", [P, 2, H1])
        w1d_sb = sb("w1d_sb", [DENSE, H1])
        w2_sb = sb("w2_sb", [P, 4, H2])
        w3_sb = sb("w3_sb", [P, 2])
        b_sb = sb("b_sb", [P, 2])
        b1_sb = sb("b1_sb", [P, 4])
        b2_sb = sb("b2_sb", [P, 2])
        dense_sb = sb("dense_sb", [P, BT, DENSE])
        dense_t = sb("dense_t", [DENSE, BATCH])
        tail = nat[:].rearrange("p f t h e -> p f (t h e)")
        z_sb, h1_sb, h2_sb = tail[:, 0:2, :], tail[:, 2:6, :], tail[:, 6:8, :]
        y_sb = tail[0:1, 0, :]

        t_ps = ctx.enter_context(nc.psum_tensor("t_ps", [P, T_BUFS, 2, BATCH], F32))
        tr_ps = ctx.enter_context(nc.psum_tensor("tr_ps", [P, BATCH], F32))
        sum_ps = ctx.enter_context(nc.psum_tensor("sum_ps", [P, BATCH], F32))

        def tile_bank(n):
            return t_ps[:, T_BUFS - 1, 1, :] if in_t_ps(n) else tr_ps[:]

        z_ps, h1_ps = t_ps[:, 2, :, :], t_ps[:, 0:2, :, :].rearrange("p n h b -> p (n h) b")
        h2_ps, y_ps = (sum_ps[:], tr_ps[:]), t_ps[0:1, 2, 0, :]

        ids_loaded = sem("ids_loaded")
        w_loaded = sem("w_loaded")
        small_loaded = sem("small_loaded")
        gathered = [sem(f"gathered{f}") for f in range(FIELDS)]
        k_loaded = [sem(f"k_loaded{s}") for s in range(RAW)]
        table_loaded = [sem(f"table_loaded{f}") for f in PICKED]
        ids_converted = sem("ids_converted")
        numbered = sem("numbered")
        constants_ready = sem("constants_ready")
        table_high_ready = sem("table_high_ready")
        table_split = sem("table_split")
        one_hot_ready = sem("one_hot_ready")
        one_hot_used = sem("one_hot_used")
        ident_ready = sem("ident_ready")
        zeroed = sem("zeroed")
        first_row_ready = sem("first_row_ready")
        zeroed_dve = sem("zeroed_dve")
        slots_ready = sem("slots_ready")
        high_ready = sem("high_ready")
        parts_ready = sem("parts_ready")
        transposed = sem("transposed")
        tile_copied = sem("tile_copied")
        k_high_ready = sem("k_high_ready")
        k_split_dve = sem("k_split_dve")
        k_split_pool = sem("k_split_pool")
        t_ready = sem("t_ready")
        multiplied = sem("multiplied")
        reduced = sem("reduced")
        pij_copied = sem("pij_copied")
        pij_added = sem("pij_added")
        z_ready = sem("z_ready")
        z_copied = sem("z_copied")
        z_copied_dve = sem("z_copied_dve")
        h1_ready = sem("h1_ready")
        h1_even = sem("h1_even")
        h1_odd = sem("h1_odd")
        h2_ready = sem("h2_ready")
        h2_even = sem("h2_even")
        h2_odd = sem("h2_odd")
        y_ready = sem("y_ready")
        y_copied = sem("y_copied")
        stored = sem("stored")

        def loads_of(q, r):
            for h in range(2):
                i = 4 * r + 2 * h
                c = 0 if r < q else 2 * h + 1
                at = pair_index(i, QUAD * q + c)
                yield 2 * h, c, QUAD - c, bass.AP(
                    kern.tensor, at * DIM,
                    [[PAIRS * DIM, DIM], [(FIELDS - 2 - i) * DIM, 2], [1, (QUAD - c) * DIM]])

        def wait_split(engine, n):
            if n < POOL_FROM:
                engine.wait_ge(k_split_dve, n + 1)
            else:
                engine.wait_ge(k_split_pool, n - POOL_FROM + 1)

        def wait_sums(engine, q):
            if q in ADDED:
                engine.wait_ge(pij_added, ADDED.index(q) + 1)
            else:
                engine.wait_ge(pij_copied, q + 1)

        def wait_used(engine, m):
            f, c = [(f, c) for f in PICKED for c in range(cuts[f])][m]
            if c == cuts[f] - 1:
                engine.wait_ge(transposed, TILE["moving", f] + 1)
            else:
                engine.wait_ge(one_hot_used, m + 1 - PICKED.index(f))

        def nat_of(f):
            return nat[:, f // 2 % (2 * NAT_QUADS), :, f % 2, :]

        def k_views(n, row, c):
            raw = k_raw[:, n % RAW, row:row + 2, c * DIM:].rearrange("p r (c e) -> p r c e", e=DIM)
            return raw, *(x[:, n % SPLIT, row // 2, c:, :].rearrange("p c (r e) -> p r c e", r=2) for x in (k_high, k_low))

        block = ctx.enter_context(nc.Block())


        @block.sync
        def _(sp):
            sp.dma_start(ids_sb[:], ids.rearrange("(t p) f -> p t f", p=P)).then_inc(ids_loaded, 16)
            for n, f in enumerate(PICKED):
                sp.dma_start(table_raw[0:rows_of[f], n, 0:cuts[f], :],
                             tables[f].rearrange("(p c) e -> p c e", c=cuts[f])).then_inc(table_loaded[n], 16)
            for n, (q, r) in enumerate(PIECES):
                if n == RAW:
                    sp.dma_start(w_sb[:], w.rearrange("(p c) n -> p c n", p=P)).then_inc(w_loaded, 16)
                    small = [(dense_sb, dense.rearrange("(t p) n -> p t n", p=P)),
                             (w1_sb, w1[0:Z_OUT, :].rearrange("(p c) n -> p c n", p=P)),
                             (w1d_sb, w1[Z_OUT:Z_OUT + DENSE, :]),
                             (w2_sb, w2.rearrange("(p c) n -> p c n", p=P)),
                             (w3_sb, w3.rearrange("(p c) o -> p (c o)", p=P)),
                             (b_sb, b.rearrange("(p c) -> p c", p=P)),
                             (b1_sb, b1.rearrange("(p c) -> p c", p=P)),
                             (b2_sb, b2.rearrange("(p c) -> p c", p=P))]
                    for to, of in small:
                        sp.dma_start(to[:], of).then_inc(small_loaded, 16)
                if n >= RAW:
                    wait_split(sp, n - RAW)
                for row, c, _, view in loads_of(q, r):
                    for half in range(2):
                        sp.dma_start(k_raw[DIM * half:DIM * half + DIM, n % RAW, row:row + 2, c * DIM:],
                                     view).then_inc(k_loaded[n % RAW], 16)
            sp.wait_ge(y_copied, 1)
            sp.dma_start(out.rearrange("b o -> o b"), y_sb).then_inc(stored, 16)
            sp.wait_ge(stored, 16)

        @block.gpsimd
        def _(pool):
            nc.gpsimd.memset(ident[:], 0.0).then_inc(zeroed, 1)
            pool.wait_ge(zeroed, 1)
            nc.gpsimd.affine_select(out=ident[:], in_=ident[:], compare_op=ALU.not_equal, fill=1.0, base=0,
                                    pattern=[[-1, P]], channel_multiplier=1).then_inc(ident_ready, 1)
            for n, f in enumerate(PICKED):
                last = nc.gpsimd.iota(first_row_i[:, n:n + 1], pattern=[[0, 1]], base=0, channel_multiplier=cuts[f])
            last.then_inc(numbered, 1)
            pool.wait_ge(ids_loaded, 16)
            for f in GATHERED:
                if f >= NAT_QUADS * QUAD and f % QUAD == 0:
                    done = range((f - QUAD * NAT_QUADS) // 2 + 2)
                    pool.wait_ge(transposed, max(TILE["factor", k] for k in done) + 1)
                for t in range(BT):
                    nc.gpsimd.indirect_dma_start(
                        nat[:, f // 2 % (2 * NAT_QUADS), t, f % 2, :], None, tables[f],
                        bass.IndirectOffsetOnAxis(ap=ids_sb[:, t, f:f + 1].bitcast(U32), axis=0),
                    ).then_inc(gathered[f], 16)
            nc.gpsimd.memset(w_slots[:], 0.0).then_inc(zeroed, 1)
            for n in range(POOL_FROM, len(PIECES)):
                pool.wait_ge(k_high_ready, n + 1)
                for row, c, _, _ in loads_of(*PIECES[n]):
                    raw, high, low = k_views(n, row, c)
                    last = nc.gpsimd.tensor_tensor(low, raw, high, ALU.subtract)
                last.then_inc(k_split_pool, 1)
                if n == POOL_FROM:
                    pool.wait_ge(zeroed, 2)
                    pool.wait_ge(w_loaded, 16)
                for i in range(W_ROWS * (n - POOL_FROM), min(W_ROWS * (n - POOL_FROM + 1), FIELDS - 1)):
                    for q in range(i // QUAD, QUADS):
                        c = i % QUAD + 1 if q == i // QUAD else 0
                        if c == QUAD or (q > QUADS // 2 and c == 0 and q > i // QUAD + 1):
                            continue
                        at = pair_index(i, QUAD * q + c)
                        if q >= QUADS // 2 and c == 0:
                            quads = QUADS - q
                            for h in range(2):
                                last = nc.gpsimd.tensor_copy(
                                    w_slots[:, h, CHUNK[q]:CHUNK[q] + quads, :, i],
                                    w_sb[:, h, at:at + quads * QUAD].rearrange("p (n k) -> p n k", k=QUAD))
                        else:
                            last = nc.gpsimd.tensor_copy(w_slots[:, :, CHUNK[q], c:, FIRST_ROW[q] + i],
                                                         w_sb[:, :, at:at + QUAD - c])
                    if i == FIELDS - 2:
                        last.then_inc(slots_ready, 1)

        @block.scalar
        def _(act):
            def split_high(n):
                q, r = PIECES[n]
                act.wait_ge(k_loaded[n % RAW], 64 * (n // RAW + 1))
                if n >= SPLIT:
                    act.wait_ge(t_ready, 2 * GROUPS_TO_PIECE[n - SPLIT])
                for row, c, _, _ in loads_of(q, r):
                    raw, high, _ = k_views(n, row, c)
                    last = nc.scalar.copy(high, raw)
                last.then_inc(k_high_ready, 1)

            def copy_tile(tile):
                kind, x = tile
                n = TILE[tile]
                of = tile_bank(n)
                act.wait_ge(transposed, n + 1)
                if kind == "ids":
                    to, of = ids_t[:], of[0:FIELDS, :]
                elif kind == "index":
                    to = index[:, PICKED.index(x), :]
                elif kind == "w":
                    to = w_t[:, BATCH * x:min(BATCH * (x + 1), CHUNKS * Z_OUT)]
                    of = of[:, 0:to.shape[1]]
                elif kind == "dense":
                    to, of = dense_t[:], of[0:DENSE, :]
                elif kind == "moving":
                    q = x // QUAD
                    if q >= 2:
                        act.wait_ge(t_ready, 2 * GROUPS_BEFORE_QUAD[q - 1])
                    to = moving[:, q % 2, x % QUAD, :]
                else:
                    to = factor[:, x, :]
                nc.scalar.copy(to, of).then_inc(tile_copied, 1)

            def high_part(f):
                act.wait_ge(gathered[f], 16 * BT)
                if f >= 2 * QUAD:
                    act.wait_ge(transposed, TILE["moving", f - 2 * QUAD] + 1)
                nc.scalar.copy(parts[:, f % (2 * QUAD), :, 0, :], nat_of(f)).then_inc(high_ready, 1)

            def copy_sums(q):
                act.wait_ge(reduced, GROUPS_BEFORE_QUAD[q + 1])
                if q == 0:
                    for c in range(1, QUAD):
                        last = nc.scalar.copy(pij[32 * c:32 * c + 32, CHUNK[0], :], sum_ps[32 * c:32 * c + 32, :])
                elif q in ADDED:
                    if q - 1 in ADDED:
                        act.wait_ge(pij_added, ADDED.index(q))
                    last = nc.scalar.copy(late_sums[:], sum_ps[:])
                else:
                    last = nc.scalar.copy(pij[:, CHUNK[q], :], sum_ps[:])
                last.then_inc(pij_copied, 1)

            def table_high(n):
                f = PICKED[n]
                act.wait_ge(table_loaded[n], 16)
                if n >= 2:
                    act.wait_ge(transposed, TILE["moving", PICKED[n - 2]] + 1)
                nc.scalar.copy(table_parts[0:rows_of[f], n % 2, 0:cuts[f], 0, :],
                               table_raw[0:rows_of[f], n, 0:cuts[f], :]).then_inc(table_high_ready, 1)

            for tile in TILES[:1 + len(PICKED)]:
                copy_tile(tile)
            table_high(0)
            table_high(1)
            high_part(0)
            split_high(0)
            copy_tile(("moving", 3))
            copy_tile(("moving", 0))
            high_part(1)
            table_high(2)
            copy_tile(("moving", 6))
            high_part(2)
            copy_tile(("moving", 1))
            copy_tile(("factor", 0))
            copy_tile(("moving", 2))
            split_high(1)
            copy_tile(("factor", 1))
            high_part(4)
            copy_tile(("moving", 7))
            copy_tile(("factor", 3))
            copy_tile(("moving", 4))
            high_part(5)
            for n, (q, r) in enumerate(PIECES):
                if n + AHEAD < len(PIECES):
                    split_high(n + AHEAD)
                for g, (piece, *_) in enumerate(GROUPS):
                    if piece == n:
                        if q and g == GROUPS_BEFORE_QUAD[q]:
                            copy_sums(q - 1)
                        tiles = TILES_AFTER.get(g, [])
                        late = [f for f in fields_after(g) if ("moving", f) in tiles]
                        for tile in tiles:
                            if tile[0] == "moving" and tile[1] in late:
                                high_part(tile[1])
                            copy_tile(tile)
                        for f in fields_after(g):
                            if f not in late:
                                high_part(f)
            copy_sums(QUADS - 1)

            act.wait_ge(small_loaded, 16 * SMALL)
            act.wait_ge(z_ready, 1)
            nc.scalar.activation(z_sb[:, 0, :], z_ps[:, 0, :], ACT.Identity, bias=b_sb[:, 0:1]).then_inc(z_copied, 1)
            for n in (0, 2):
                act.wait_ge(h1_ready, n + 1)
                nc.scalar.activation(h1_sb[:, n, :], h1_ps[:, n, :], ACT.Relu,
                                     bias=b1_sb[:, n:n + 1]).then_inc(h1_even, 1)
            act.wait_ge(h2_ready, 1)
            nc.scalar.activation(h2_sb[:, 0, :], h2_ps[0], ACT.Relu, bias=b2_sb[:, 0:1]).then_inc(h2_even, 1)
            act.wait_ge(y_ready, 1)
            nc.scalar.copy(y_sb, y_ps).then_inc(y_copied, 1)

        @block.vector
        def _(dve):
            def split_low(n):
                q, r = PIECES[n]
                dve.wait_ge(k_high_ready, n + 1)
                for row, c, _, _ in loads_of(q, r):
                    raw, high, low = k_views(n, row, c)
                    last = nc.vector.tensor_tensor(low, raw, high, ALU.subtract)
                last.then_inc(k_split_dve, 1)

            def low_part(f):
                dve.wait_ge(high_ready, GATHERED.index(f) + 1)
                high = parts[:, f % (2 * QUAD), :, 0, :]
                nc.vector.tensor_tensor(parts[:, f % (2 * QUAD), :, 1, :], nat_of(f), high,
                                        ALU.subtract).then_inc(parts_ready, 1)

            def add_sums(q):
                dve.wait_ge(pij_copied, q + 1)
                nc.vector.tensor_tensor(pij[:, CHUNK[q], :], late_sums[:], pij[:, CHUNK[q], :],
                                        ALU.add).then_inc(pij_added, 1)

            def multiply(g, half):
                _, q, r, batches = GROUPS[g]
                kind, units = batches[half]
                n = 2 * g + half
                k = units[0][0]
                dve.wait_ge(t_ready, n + 1)
                if half == 0 or kind == SINGLE:
                    dve.wait_ge(tile_copied, TILE["factor", k + (kind == SINGLE)] + 1)
                if kind == FULL:
                    if n >= PRODUCTS:
                        dve.wait_ge(reduced, (n - PRODUCTS) // 2 + 1)
                    nc.vector.tensor_tensor(prod[:, n % PRODUCTS, :, :], t_ps[:, n % T_BUFS, :, :],
                                            factor[:, k:k + 1, :].broadcast_to([P, 2, BATCH]),
                                            ALU.mult).then_inc(multiplied, 1)
                else:
                    if q:
                        dve.wait_ge(reduced, GROUPS_BEFORE_QUAD[q])
                    nc.vector.tensor_tensor(prod1[0:DIM, :, :], t_ps[0:DIM, n % T_BUFS, :, :],
                                            factor[0:DIM, k:k + 2, :], ALU.mult).then_inc(multiplied, 1)

            dve.wait_ge(ids_loaded, 16)
            nc.vector.tensor_copy(ids_f[:], ids_sb[:]).then_inc(ids_converted, 1)
            dve.wait_ge(ident_ready, 1)
            for n, f in enumerate(PICKED):
                last = nc.vector.tensor_copy(row_pick[:, n, :], ident[0:FIELDS, f:f + 1].broadcast_to([FIELDS, P]))
            last.then_inc(constants_ready, 1)
            dve.wait_ge(numbered, 1)
            nc.vector.tensor_copy(first_row[:], first_row_i[:]).then_inc(first_row_ready, 1)
            dve.wait_ge(first_row_ready, 1)
            nc.vector.memset(add_halves[:].bitcast(F32), 0.0)
            nc.vector.memset(select[:], 0.0).then_inc(zeroed_dve, 1)
            dve.wait_ge(zeroed_dve, 1)
            for h in range(2):
                side = slice(DIM * h, DIM * h + DIM)
                last = nc.vector.tensor_copy(add_halves[side, DIM:2 * DIM], ident[side, side])
            last.then_inc(constants_ready, 1)
            nc.vector.memset(select[0:DIM, 30:31], 1.0)
            nc.vector.memset(select[DIM:P, 31:32], 1.0)
            nc.vector.memset(pij[0:32, CHUNK[0], :], 0.0)
            nc.vector.memset(prod1[DIM:P, :, :], 0.0)

            def make_one_hots(n):
                f = PICKED[n]
                rows = rows_of[f]
                dve.wait_ge(table_high_ready, n + 1)
                nc.vector.tensor_tensor(table_parts[0:rows, n % 2, 0:cuts[f], 1, :], table_raw[0:rows, n, 0:cuts[f], :],
                                        table_parts[0:rows, n % 2, 0:cuts[f], 0, :],
                                        ALU.subtract).then_inc(table_split, 1)
                dve.wait_ge(tile_copied, TILE["index", f] + 1)
                for c in range(cuts[f]):
                    made = sum(cuts[x] for x in PICKED[:n]) + c
                    if made >= ONE_HOTS:
                        wait_used(dve, made - ONE_HOTS)
                    nc.vector.tensor_scalar(one_hot[made % ONE_HOTS][0:rows, :], index[0:rows, n, :], float(c),
                                            first_row[0:rows, n:n + 1], ALU.subtract, ALU.is_equal).then_inc(one_hot_ready, 1)

            make_one_hots(0)
            low_part(0)
            make_one_hots(1)
            low_part(1)
            low_part(2)
            split_low(0)
            make_one_hots(2)
            split_low(1)
            low_part(4)
            low_part(5)
            multiply(0, 0)
            multiply(0, 1)
            g = 0
            for n, (q, r) in enumerate(PIECES):
                for start in (True, False)[:len(groups_of(q, r))]:
                    if g:
                        multiply(g, 0)
                        multiply(g, 1)
                    for f in fields_after(g):
                        low_part(f)
                    if start and n + AHEAD < POOL_FROM:
                        split_low(n + AHEAD)
                    if q and g - 3 == GROUPS_BEFORE_QUAD[q] and q - 1 in ADDED:
                        add_sums(q - 1)
                    g += 1

            dve.wait_ge(small_loaded, 16 * SMALL)
            dve.wait_ge(z_ready, 2)
            nc.vector.tensor_scalar(z_sb[:, 1, :], z_ps[:, 1, :], b_sb[:, 1:2], None, ALU.add).then_inc(z_copied_dve, 1)
            for n in (1, 3):
                dve.wait_ge(h1_ready, n + 1)
                nc.vector.tensor_scalar(h1_sb[:, n, :], h1_ps[:, n, :], b1_sb[:, n:n + 1], 0.0,
                                        ALU.add, ALU.max).then_inc(h1_odd, 1)
            dve.wait_ge(h2_ready, 2)
            nc.vector.tensor_scalar(h2_sb[:, 1, :], h2_ps[1], b2_sb[:, 1:2], 0.0,
                                    ALU.add, ALU.max).then_inc(h2_odd, 1)

        @block.tensor
        def _(pe):
            def free_tile(n):
                earlier = [m for m in range(n) if in_t_ps(m) == in_t_ps(n)]
                if earlier:
                    pe.wait_ge(tile_copied, earlier[-1] + 1)

            def make_tile(tile):
                kind, x = tile
                n = TILE[tile]
                free_tile(n)
                if kind == "ids":
                    pe.wait_ge(ids_converted, 1)
                elif kind == "moving":
                    pe.wait_ge(parts_ready, GATHERED.index(x) + 1)
                elif kind == "w":
                    pe.wait_ge(slots_ready, 1)
                elif kind == "dense":
                    pe.wait_ge(small_loaded, 16 * SMALL)
                for s in range(4):
                    rows = P
                    if kind == "w":
                        chunk, c = (4 * x + s) // 2, s % 2
                        if chunk == CHUNKS:
                            break
                        of = w_slots[:, c, chunk, :, :].rearrange("p k i -> p (k i)")
                    elif kind == "dense":
                        of, rows = dense_sb[:, s, :], DENSE
                    elif kind == "ids":
                        of, rows = ids_f[:, s, :], FIELDS
                    elif kind == "moving":
                        of = parts[:, x % (2 * QUAD), s, :, :].bitcast(F32).rearrange("p h e -> p (h e)")
                    else:
                        of = nat[:, x % (2 * NAT_QUADS), s, :, :].rearrange("p h e -> p (h e)")
                    last = nc.tensor.transpose(tile_bank(n)[0:rows, P * s:P * s + P], of, ident[:])
                last.then_inc(transposed, 1)

            def make_index(f):
                n = TILE["index", f]
                pe.wait_ge(constants_ready, 1)
                pe.wait_ge(tile_copied, 1)
                free_tile(n)
                nc.tensor.matmul(tile_bank(n), row_pick[:, PICKED.index(f), :], ids_t[:], start=True,
                                 stop=True).then_inc(transposed, 1)

            def pick(f):
                n = PICKED.index(f)
                made = sum(cuts[x] for x in PICKED[:n])
                pe.wait_ge(table_split, n + 1)
                free_tile(TILE["moving", f])
                for c in range(cuts[f]):
                    pe.wait_ge(one_hot_ready, made + c + 1)
                    one = nc.tensor.matmul(
                        tile_bank(TILE["moving", f]), table_parts[0:rows_of[f], n % 2, c, :, :].rearrange("p h e -> p (h e)"),
                        one_hot[(made + c) % ONE_HOTS][0:rows_of[f], :],
                        start=c == 0, stop=c == cuts[f] - 1)
                    one.then_inc(one_hot_used if c < cuts[f] - 1 else transposed, 1)

            def add_parts(k):
                n = TILE["factor", k]
                pe.wait_ge(constants_ready, 2)
                free_tile(n)
                pe.wait_ge(tile_copied, max([0] + [TILE["moving", f] + 1 for f in (2 * k, 2 * k + 1)]))
                for h in range(2):
                    f = 2 * k + h
                    last = nc.tensor.matmul(tile_bank(n), add_halves[:, DIM * (1 - h):DIM * (1 - h) + P],
                                            moving[:, f // QUAD % 2, f % QUAD, :], start=h == 0, stop=h == 1)
                last.then_inc(transposed, 1)

            def make(tile):
                if tile[0] == "factor" and {2 * tile[1], 2 * tile[1] + 1} & set(PICKED):
                    add_parts(tile[1])
                elif tile[0] == "moving" and tile[1] in PICKED:
                    pick(tile[1])
                else:
                    make_tile(tile)

            def contract(g):
                n, q, r, batches = GROUPS[g]
                first_of_piece = g == 0 or GROUPS[g - 1][0] != n
                if first_of_piece:
                    wait_split(pe, n)
                    pe.wait_ge(tile_copied, FIELDS_DONE[q])
                for half, (_, units) in enumerate(batches):
                    batch = 2 * g + half
                    if batch >= T_BUFS:
                        pe.wait_ge(multiplied, batch - T_BUFS + 1)
                    for u, (k, c) in enumerate(units):
                        for which, part in enumerate((k_high, k_low)):
                            last = nc.tensor.matmul(t_ps[:, batch % T_BUFS, u, :],
                                                    part[:, n % SPLIT, k - 2 * r, c, :],
                                                    moving[:, q % 2, c, :],
                                                    start=which == 0, stop=which == 1)
                    last.then_inc(t_ready, 1)

            def reduce(g):
                _, q, r, batches = GROUPS[g]
                if g == GROUPS_BEFORE_QUAD[q] and q:
                    pe.wait_ge(pij_copied, q)
                pe.wait_ge(multiplied, 2 * g + 2)
                for half, (kind, units) in enumerate(batches):
                    for u, (k, c) in enumerate(units):
                        of = prod[:, (2 * g + half) % PRODUCTS, u, :] if kind == FULL else prod1[:, u, :]
                        last = nc.tensor.matmul(sum_ps[32 * c:32 * c + 32, :],
                                                select[:, 30 - 2 * k - FIRST_ROW[q]:62 - 2 * k - FIRST_ROW[q]], of,
                                                start=k == 0, stop=k == LAST_UNIT[q, c])
                last.then_inc(reduced, 1)

            pe.wait_ge(ident_ready, 1)
            make(("ids", 0))
            for f in PICKED:
                make_index(f)
            for tile in FIRST_TILES[1 + len(PICKED):]:
                make(tile)
            for g in range(len(GROUPS)):
                contract(g)
                for done in reductions_after(g):
                    reduce(done)
                for tile in TILES_AFTER.get(g, []):
                    make(tile)

            def add_z(c, chunk, start, stop):
                at = chunk * Z_OUT + P * c
                return nc.tensor.matmul(z_ps[:, c, :], w_t[:, at:at + P], pij[:, chunk, :], start=start, stop=stop)

            pe.wait_ge(multiplied, 2 * len(GROUPS) - 2)
            wait_sums(pe, 3)
            wait_sums(pe, 6)
            early = [chunk for chunk in range(CHUNKS) if chunk != CHUNK[QUADS - 1]]
            for c in range(2):
                for chunk in early:
                    add_z(c, chunk, chunk == early[0], False)
            reduce(len(GROUPS) - 1)
            pe.wait_ge(multiplied, 2 * len(GROUPS))
            pe.wait_ge(tile_copied, len(TILES))
            def add_dense(n):
                nc.tensor.matmul(h1_ps[:, n, :], w1d_sb[:, n::4], dense_t[:], start=True, stop=False)

            add_dense(0)
            wait_sums(pe, QUADS - 1)
            for c in range(2):
                add_z(c, CHUNK[QUADS - 1], False, True).then_inc(z_ready, 1)
            for n in range(1, 4):
                add_dense(n)
            pe.wait_ge(z_copied, 1)
            pe.wait_ge(z_copied_dve, 1)
            for n in range(4):
                for c in range(2):
                    last = nc.tensor.matmul(h1_ps[:, n, :], w1_sb[:, c, n::4], z_sb[:, c, :],
                                            start=False, stop=c == 1)
                last.then_inc(h1_ready, 1)
            for c in range(4):
                pe.wait_ge(h1_odd if c % 2 else h1_even, c // 2 + 1)
                for n in range(2):
                    if c == 0 and n == 1:
                        pe.wait_ge(tile_copied, len(TILES))
                    last = nc.tensor.matmul(h2_ps[n], w2_sb[:, c, n::2], h1_sb[:, c, :],
                                            start=c == 0, stop=c == 3)
                    if c == 3:
                        last.then_inc(h2_ready, 1)
            for c in range(2):
                pe.wait_ge(h2_odd if c else h2_even, 1)
                last = nc.tensor.matmul(y_ps, w3_sb[:, c:c + 1], h2_sb[:, c, :], start=c == 0, stop=c == 1)
            last.then_inc(y_ready, 1)


_TABLES = [f"tbl_{f}" for f in range(FIELDS)]
_INS = ["dense_ctx", "ids"] + _TABLES + ["W_top1", "b_top1", "W_top2", "b_top2", "W_top3",
                                          "L0_rec_kernel", "L0_rec_W", "L0_rec_b"]


def kernel(**inputs):
    import numpy as _np
    import concourse.bacc as _bacc
    from concourse import mybir as _mybir
    from concourse.bass_utils import run_bass_kernel_spmd as _run

    nc = _bacc.Bacc("TRN2", target_bir_lowering=False, num_devices=1)
    arrays, args = {}, {}
    for name in _INS:
        a = _np.ascontiguousarray(inputs[name])
        arrays[f"in_{name}"] = a
        args[name] = nc.dram_tensor(f"in_{name}", a.shape, _mybir.dt.from_np(a.dtype), kind="ExternalInput").ap()
    out = nc.dram_tensor("out_y", (BATCH, 1), _mybir.dt.float32, kind="ExternalOutput").ap()
    build(nc, args["dense_ctx"], args["ids"], [args[t] for t in _TABLES], args["W_top1"], args["b_top1"],
          args["W_top2"], args["b_top2"], args["W_top3"], args["L0_rec_kernel"], args["L0_rec_W"],
          args["L0_rec_b"], out)
    r = _run(nc, [arrays], core_ids=[0])
    return r.results[0]["out_y"]
```

```python
from contextlib import ExitStack

import concourse.bass as bass
from concourse import mybir

BATCH, FIELDS, DIM, DENSE = 512, 32, 64, 16
PAIRS = FIELDS * (FIELDS - 1) // 2
P = 128
BT = BATCH // P
QUAD = 4
QUADS = FIELDS // QUAD
Z_OUT, H1, H2 = 256, 512, 256

PIECES = [(q, r) for q in range(QUADS) for r in range(q + 1)]
FULL, SINGLE = 0, 1


def groups_of(q, r):
    if r < q:
        return [[(FULL, [(k, 0), (k, 1)]), (FULL, [(k, 2), (k, 3)])] for k in (2 * r, 2 * r + 1)]
    return [[(FULL, [(2 * r, 2), (2 * r, 3)]), (SINGLE, [(2 * r, 1), (2 * r + 1, 3)])]]


GROUPS = [(n, q, r, g) for n, (q, r) in enumerate(PIECES) for g in groups_of(q, r)]
GROUPS_BEFORE_QUAD = [sum(1 for _, q, _, _ in GROUPS if q < m) for m in range(QUADS + 1)]
GROUPS_TO_PIECE = [sum(1 for p, *_ in GROUPS if p <= n) for n in range(len(PIECES))]
LAST_UNIT = {(q, c): k for _, q, _, g in GROUPS for _, units in g for k, c in units}

RAW, SPLIT, AHEAD = 3, 3, 2
PRODUCTS = 6
T_BUFS = 3
NAT_QUADS = 4

CHUNKS = 5
CHUNK = [2, 1, 0, 4, 0, 1, 2, 3]
FIRST_ROW = [28, 24, 20, 0, 0, 0, 0, 0]
ADDED = (4, 5, 6)

PICKED = (3, 6, 7)
GATHERED = [f for f in range(FIELDS) if f not in PICKED]
POOL_BEHIND = {21: 10, 22: 12, 24: 14, 25: 15, 26: 16, 27: 17, 28: 18, 29: 19, 30: 20}
POOL_FROM = 22
POOL_PIECES = list(POOL_BEHIND.values()) + list(range(POOL_FROM, len(PIECES)))
DVE_PIECES = [n for n in range(len(PIECES)) if n not in POOL_PIECES]
LATE_FIELDS = (11,)
ONE_HOTS = 4
CUTS_MAX = 10

W_ROWS = 4
W_FROM = 54
DENSE_FROM = 40

FIRST_TILES = [("ids", 0)] + [("index", f) for f in PICKED]
FIRST_TILES += [("moving", 3), ("moving", 0), ("moving", 6), ("moving", 1), ("factor", 0), ("moving", 2),
                ("factor", 1), ("moving", 7), ("factor", 3), ("moving", 4)]
TILES_AFTER = {0: [("moving", 5), ("factor", 2)],
               1: [("moving", 8)],
               2: [("moving", 9), ("factor", 4)],
               3: [("moving", 10), ("moving", 11), ("factor", 5)],
               5: [("moving", 12)],
               6: [("moving", 13)],
               7: [("factor", 6), ("moving", 14)],
               8: [("moving", 15), ("factor", 7)]}
for _q in range(3, QUADS - 1):
    _f = QUAD * (_q + 1)
    _tiles = [("moving", _f), ("moving", _f + 1), ("factor", _f // 2),
              ("moving", _f + 2), ("moving", _f + 3), ("factor", _f // 2 + 1)]
    _groups = range(GROUPS_BEFORE_QUAD[_q], GROUPS_BEFORE_QUAD[_q + 1])[-len(_tiles):]
    for _n, _tile in enumerate(_tiles):
        TILES_AFTER.setdefault(_groups[_n * len(_groups) // len(_tiles)], []).append(_tile)
for _n, _tile in enumerate([("w", n) for n in range((2 * CHUNKS + 3) // 4)] + [("dense", 0)]):
    TILES_AFTER.setdefault(W_FROM + _n, []).append(_tile)
TILES = FIRST_TILES + [tile for g in range(len(GROUPS)) for tile in TILES_AFTER.get(g, [])]
TILE = {tile: n for n, tile in enumerate(TILES)}
FIELDS_DONE = [max(TILE["moving", f] for f in range(QUAD * q, QUAD * q + QUAD)) + 1 for q in range(QUADS)]


def fields_after(g):
    return [x for n in (g, g + 1) for kind, x in TILES_AFTER.get(n, [])
            if kind == "moving" and (x in LATE_FIELDS) == (n == g)]


def in_t_ps(n):
    return n % 2 == 1 and n < FIELDS_DONE[1]


def pair_index(i, j):
    return i * FIELDS - i * (i + 1) // 2 + j - i - 1


def build(nc, dense, ids, tables, w1, b1, w2, b2, w3, kern, w, b, out):
    F32, F32R, I32, U32 = mybir.dt.float32, mybir.dt.float32r, mybir.dt.int32, mybir.dt.uint32
    ALU, ACT = mybir.AluOpType, mybir.ActivationFunctionType
    with ExitStack() as ctx:
        def sb(name, shape, dt=F32):
            return ctx.enter_context(nc.sbuf_tensor(name, shape, dt))

        def sem(name):
            return ctx.enter_context(nc.semaphore(name))

        ids_sb = sb("ids_sb", [P, BT, FIELDS], I32)
        nat = sb("nat", [P, NAT_QUADS * 2, BT, 2, DIM])
        parts = sb("parts", [P, 2 * QUAD, BT, 2, DIM], F32R)
        moving = sb("moving", [P, 2, QUAD, BATCH], F32R)
        factor = sb("factor", [P, FIELDS // 2, BATCH])
        k_raw = sb("k_raw", [P, RAW, QUAD, QUAD * DIM])
        k_high = sb("k_high", [P, SPLIT, 2, QUAD, 2 * DIM], F32R)
        k_low = sb("k_low", [P, SPLIT, 2, QUAD, 2 * DIM], F32R)
        prod = sb("prod", [P, PRODUCTS, 2, BATCH])
        prod1 = sb("prod1", [P, 2, BATCH])
        select = sb("select", [P, 62])
        ident = sb("ident", [P, P])
        pij = sb("pij", [P, CHUNKS, BATCH])
        w_sb = sb("w_sb", [P, 2, PAIRS])
        w_t = sb("w_t", [P, CHUNKS * Z_OUT])
        w_slots = sb("w_slots", [P, 2, CHUNKS, QUAD, FIELDS])
        prod_flat = prod[:].rearrange("p n h b -> p (n h b)")
        cuts = {f: next(c for c in range(1, CUTS_MAX + 1) if tables[f].shape[0] % c == 0 and tables[f].shape[0] // c <= P)
                for f in PICKED}
        rows_of = {f: tables[f].shape[0] // cuts[f] for f in PICKED}
        index_at = 2 * BATCH
        table_at = index_at + len(PICKED) * BATCH
        index = prod_flat[:, index_at:table_at].rearrange("p (n b) -> p n b", b=BATCH)
        table_raw = prod_flat[:, table_at:table_at + len(PICKED) * CUTS_MAX * DIM].rearrange(
            "p (n c e) -> p n c e", n=len(PICKED), e=DIM)
        table_parts = sb("table_parts", [P, 2, CUTS_MAX, 2, DIM], F32R)
        one_hot_ring = sb("one_hot_ring", [P, ONE_HOTS, BATCH], F32R)
        one_hot = [one_hot_ring[:, n, :] for n in range(ONE_HOTS)]
        dense_t, w1d_parts = one_hot[0], one_hot[1]
        dense_parts = one_hot[2].rearrange("p (t s n) -> p t s n", t=BT, n=32)
        ids_f = sb("ids_f", [P, BT, FIELDS])
        ids_t = sb("ids_t", [FIELDS, BATCH], F32R)
        row_pick = sb("row_pick", [FIELDS, len(PICKED), P], F32R)
        first_row = sb("first_row", [P, len(PICKED)])
        first_row_i = sb("first_row_i", [P, len(PICKED)], I32)
        add_halves = sb("add_halves", [P, 3 * DIM], F32R)
        late_sums = sb("late_sums", [P, BATCH])
        w1_sb = sb("w1_sb", [P, 2, H1])
        w1d_sb = sb("w1d_sb", [P, H1])
        w2_sb = sb("w2_sb", [P, 4, H2])
        w3_sb = sb("w3_sb", [P, 2])
        b_sb = sb("b_sb", [P, 2])
        b1_sb = sb("b1_sb", [P, 4])
        b2_sb = sb("b2_sb", [P, 2])
        dense_sb = sb("dense_sb", [P, BT, DENSE])
        tail = nat[:].rearrange("p f t h e -> p f (t h e)")
        z_sb, h1_sb, h2_sb = tail[:, 0:2, :], tail[:, 2:6, :], tail[:, 6:8, :]
        y_sb = tail[0:1, 0, :]

        t_ps = ctx.enter_context(nc.psum_tensor("t_ps", [P, T_BUFS, 2, BATCH], F32))
        tr_ps = ctx.enter_context(nc.psum_tensor("tr_ps", [P, BATCH], F32))
        sum_ps = ctx.enter_context(nc.psum_tensor("sum_ps", [P, BATCH], F32))

        def tile_bank(n):
            return t_ps[:, T_BUFS - 1, 1, :] if in_t_ps(n) else tr_ps[:]

        z_ps, h1_ps = t_ps[:, 2, :, :], t_ps[:, 0:2, :, :].rearrange("p n h b -> p (n h) b")
        h2_ps, y_ps = (sum_ps[:], tr_ps[:]), t_ps[0:1, 2, 0, :]

        ids_loaded = sem("ids_loaded")
        w_loaded = sem("w_loaded")
        small_loaded = sem("small_loaded")
        gathered = [sem(f"gathered{f}") for f in range(FIELDS)]
        k_loaded = [sem(f"k_loaded{s}") for s in range(RAW)]
        table_loaded = [sem(f"table_loaded{f}") for f in PICKED]
        ids_converted = sem("ids_converted")
        numbered = sem("numbered")
        constants_ready = sem("constants_ready")
        table_high_ready = sem("table_high_ready")
        table_split = sem("table_split")
        one_hot_ready = sem("one_hot_ready")
        one_hot_used = sem("one_hot_used")
        ident_ready = sem("ident_ready")
        zeroed = sem("zeroed")
        first_row_ready = sem("first_row_ready")
        zeroed_dve = sem("zeroed_dve")
        slots_ready = sem("slots_ready")
        dense_zeroed = sem("dense_zeroed")
        dense_high = sem("dense_high")
        dense_split = sem("dense_split")
        high_ready = sem("high_ready")
        parts_ready = sem("parts_ready")
        transposed = sem("transposed")
        tile_copied = sem("tile_copied")
        k_high_ready = sem("k_high_ready")
        k_split_dve = sem("k_split_dve")
        k_split_pool = sem("k_split_pool")
        t_ready = sem("t_ready")
        multiplied = sem("multiplied")
        reduced = sem("reduced")
        pij_copied = sem("pij_copied")
        pij_added = sem("pij_added")
        z_ready = sem("z_ready")
        z_copied = sem("z_copied")
        z_copied_dve = sem("z_copied_dve")
        h1_ready = sem("h1_ready")
        h1_even = sem("h1_even")
        h1_odd = sem("h1_odd")
        h2_ready = sem("h2_ready")
        h2_even = sem("h2_even")
        h2_odd = sem("h2_odd")
        y_ready = sem("y_ready")
        y_copied = sem("y_copied")
        stored = sem("stored")

        def loads_of(q, r):
            for h in range(2):
                i = 4 * r + 2 * h
                c = 0 if r < q else 2 * h + 1
                at = pair_index(i, QUAD * q + c)
                yield 2 * h, c, QUAD - c, bass.AP(
                    kern.tensor, at * DIM,
                    [[PAIRS * DIM, DIM], [(FIELDS - 2 - i) * DIM, 2], [1, (QUAD - c) * DIM]])

        def wait_split(engine, n):
            if n in DVE_PIECES:
                engine.wait_ge(k_split_dve, DVE_PIECES.index(n) + 1)
            else:
                engine.wait_ge(k_split_pool, POOL_PIECES.index(n) + 1)

        def wait_sums(engine, q):
            if q in ADDED:
                engine.wait_ge(pij_added, ADDED.index(q) + 1)
            else:
                engine.wait_ge(pij_copied, q + 1)

        def wait_used(engine, m):
            f, c = [(f, c) for f in PICKED for c in range(cuts[f])][m]
            if c == cuts[f] - 1:
                engine.wait_ge(transposed, TILE["moving", f] + 1)
            else:
                engine.wait_ge(one_hot_used, m + 1 - PICKED.index(f))

        def nat_of(f):
            return nat[:, f // 2 % (2 * NAT_QUADS), :, f % 2, :]

        def k_views(n, row, c):
            raw = k_raw[:, n % RAW, row:row + 2, c * DIM:].rearrange("p r (c e) -> p r c e", e=DIM)
            return raw, *(x[:, n % SPLIT, row // 2, c:, :].rearrange("p c (r e) -> p r c e", r=2) for x in (k_high, k_low))

        block = ctx.enter_context(nc.Block())

        small_loads = [(dense_sb[:], dense.rearrange("(t p) n -> p t n", p=P)),
                       (w1_sb[:], w1[0:Z_OUT, :].rearrange("(p c) n -> p c n", p=P)),
                       *[(w1d_sb[32 * n:32 * n + DENSE, :], w1[Z_OUT:Z_OUT + DENSE, :]) for n in range(4)],
                       (w2_sb[:], w2.rearrange("(p c) n -> p c n", p=P)),
                       (w3_sb[:], w3.rearrange("(p c) o -> p (c o)", p=P)),
                       (b_sb[:], b.rearrange("(p c) -> p c", p=P)),
                       (b1_sb[:], b1.rearrange("(p c) -> p c", p=P)),
                       (b2_sb[:], b2.rearrange("(p c) -> p c", p=P))]

        @block.sync
        def _(sp):
            sp.dma_start(ids_sb[:], ids.rearrange("(t p) f -> p t f", p=P)).then_inc(ids_loaded, 16)
            for n, f in enumerate(PICKED):
                sp.dma_start(table_raw[0:rows_of[f], n, 0:cuts[f], :],
                             tables[f].rearrange("(p c) e -> p c e", c=cuts[f])).then_inc(table_loaded[n], 16)
            for n, (q, r) in enumerate(PIECES):
                if n == RAW:
                    sp.dma_start(w_sb[:], w.rearrange("(p c) n -> p c n", p=P)).then_inc(w_loaded, 16)
                    for to, of in small_loads:
                        sp.dma_start(to, of).then_inc(small_loaded, 16)
                if n >= RAW:
                    wait_split(sp, n - RAW)
                for row, c, _, view in loads_of(q, r):
                    for half in range(2):
                        sp.dma_start(k_raw[DIM * half:DIM * half + DIM, n % RAW, row:row + 2, c * DIM:],
                                     view).then_inc(k_loaded[n % RAW], 16)
            sp.wait_ge(y_copied, 1)
            sp.dma_start(out.rearrange("b o -> o b"), y_sb).then_inc(stored, 16)
            sp.wait_ge(stored, 16)

        @block.gpsimd
        def _(pool):
            def split_low(n):
                pool.wait_ge(k_high_ready, n + 1)
                for row, c, _, _ in loads_of(*PIECES[n]):
                    raw, high, low = k_views(n, row, c)
                    last = nc.gpsimd.tensor_tensor(low, raw, high, ALU.subtract)
                last.then_inc(k_split_pool, 1)

            nc.gpsimd.memset(ident[:], 0.0).then_inc(zeroed, 1)
            pool.wait_ge(zeroed, 1)
            nc.gpsimd.affine_select(out=ident[:], in_=ident[:], compare_op=ALU.not_equal, fill=1.0, base=0,
                                    pattern=[[-1, P]], channel_multiplier=1).then_inc(ident_ready, 1)
            for n, f in enumerate(PICKED):
                last = nc.gpsimd.iota(first_row_i[:, n:n + 1], pattern=[[0, 1]], base=0, channel_multiplier=cuts[f])
            last.then_inc(numbered, 1)
            pool.wait_ge(ids_loaded, 16)
            for f in GATHERED:
                if f >= NAT_QUADS * QUAD and f % QUAD == 0:
                    done = range((f - QUAD * NAT_QUADS) // 2 + 2)
                    pool.wait_ge(transposed, max(TILE["factor", k] for k in done) + 1)
                for t in range(BT):
                    nc.gpsimd.indirect_dma_start(
                        nat[:, f // 2 % (2 * NAT_QUADS), t, f % 2, :], None, tables[f],
                        bass.IndirectOffsetOnAxis(ap=ids_sb[:, t, f:f + 1].bitcast(U32), axis=0),
                    ).then_inc(gathered[f], 16)
                if f in POOL_BEHIND:
                    split_low(POOL_BEHIND[f])
            nc.gpsimd.memset(w_slots[:], 0.0).then_inc(zeroed, 1)
            for n in range(POOL_FROM, len(PIECES)):
                split_low(n)
                if n == POOL_FROM:
                    pool.wait_ge(zeroed, 2)
                    pool.wait_ge(w_loaded, 16)
                for i in range(W_ROWS * (n - POOL_FROM), min(W_ROWS * (n - POOL_FROM + 1), FIELDS - 1)):
                    for q in range(i // QUAD, QUADS):
                        c = i % QUAD + 1 if q == i // QUAD else 0
                        if c == QUAD or (q > QUADS // 2 and c == 0 and q > i // QUAD + 1):
                            continue
                        at = pair_index(i, QUAD * q + c)
                        if q >= QUADS // 2 and c == 0:
                            quads = QUADS - q
                            for h in range(2):
                                last = nc.gpsimd.tensor_copy(
                                    w_slots[:, h, CHUNK[q]:CHUNK[q] + quads, :, i],
                                    w_sb[:, h, at:at + quads * QUAD].rearrange("p (n k) -> p n k", k=QUAD))
                        else:
                            last = nc.gpsimd.tensor_copy(w_slots[:, :, CHUNK[q], c:, FIRST_ROW[q] + i],
                                                         w_sb[:, :, at:at + QUAD - c])
                    if i == FIELDS - 2:
                        last.then_inc(slots_ready, 1)

        @block.scalar
        def _(act):
            def split_high(n):
                q, r = PIECES[n]
                act.wait_ge(k_loaded[n % RAW], 64 * (n // RAW + 1))
                if n >= SPLIT:
                    act.wait_ge(t_ready, 2 * GROUPS_TO_PIECE[n - SPLIT])
                for row, c, _, _ in loads_of(q, r):
                    raw, high, _ = k_views(n, row, c)
                    last = nc.scalar.copy(high, raw)
                last.then_inc(k_high_ready, 1)

            def copy_tile(tile):
                kind, x = tile
                n = TILE[tile]
                of = tile_bank(n)
                act.wait_ge(transposed, n + 1)
                if kind == "ids":
                    to, of = ids_t[:], of[0:FIELDS, :]
                elif kind == "index":
                    to = index[:, PICKED.index(x), :]
                elif kind == "w":
                    to = w_t[:, BATCH * x:min(BATCH * (x + 1), CHUNKS * Z_OUT)]
                    of = of[:, 0:to.shape[1]]
                elif kind == "dense":
                    to = dense_t
                elif kind == "moving":
                    q = x // QUAD
                    if q >= 2:
                        act.wait_ge(t_ready, 2 * GROUPS_BEFORE_QUAD[q - 1])
                    to = moving[:, q % 2, x % QUAD, :]
                else:
                    to = factor[:, x, :]
                nc.scalar.copy(to, of).then_inc(tile_copied, 1)

            def high_part(f):
                act.wait_ge(gathered[f], 16 * BT)
                if f >= 2 * QUAD:
                    act.wait_ge(transposed, TILE["moving", f - 2 * QUAD] + 1)
                nc.scalar.copy(parts[:, f % (2 * QUAD), :, 0, :], nat_of(f)).then_inc(high_ready, 1)

            def copy_sums(q):
                act.wait_ge(reduced, GROUPS_BEFORE_QUAD[q + 1])
                if q == 0:
                    for c in range(1, QUAD):
                        last = nc.scalar.copy(pij[32 * c:32 * c + 32, CHUNK[0], :], sum_ps[32 * c:32 * c + 32, :])
                elif q in ADDED:
                    if q - 1 in ADDED:
                        act.wait_ge(pij_added, ADDED.index(q))
                    last = nc.scalar.copy(late_sums[:], sum_ps[:])
                else:
                    last = nc.scalar.copy(pij[:, CHUNK[q], :], sum_ps[:])
                last.then_inc(pij_copied, 1)

            def table_high(n):
                f = PICKED[n]
                act.wait_ge(table_loaded[n], 16)
                if n >= 2:
                    act.wait_ge(transposed, TILE["moving", PICKED[n - 2]] + 1)
                nc.scalar.copy(table_parts[0:rows_of[f], n % 2, 0:cuts[f], 0, :],
                               table_raw[0:rows_of[f], n, 0:cuts[f], :]).then_inc(table_high_ready, 1)

            def dense_high_parts():
                act.wait_ge(small_loaded, 16 * len(small_loads))
                act.wait_ge(dense_zeroed, 1)
                for part in (0, 2):
                    nc.scalar.copy(dense_parts[:, :, part, 0:DENSE], dense_sb[:])
                for part in range(4):
                    rows = slice(32 * part, 32 * part + DENSE)
                    last = nc.scalar.copy(w1d_parts[rows, :], w1d_sb[rows, :])
                last.then_inc(dense_high, 1)

            for tile in FIRST_TILES[:1 + len(PICKED)]:
                copy_tile(tile)
            table_high(0)
            table_high(1)
            high_part(0)
            split_high(0)
            copy_tile(("moving", 3))
            copy_tile(("moving", 0))
            high_part(1)
            table_high(2)
            copy_tile(("moving", 6))
            high_part(2)
            copy_tile(("moving", 1))
            copy_tile(("factor", 0))
            copy_tile(("moving", 2))
            split_high(1)
            copy_tile(("factor", 1))
            high_part(4)
            copy_tile(("moving", 7))
            high_part(5)
            copy_tile(("factor", 3))
            copy_tile(("moving", 4))
            for n, (q, r) in enumerate(PIECES):
                if n + AHEAD < len(PIECES):
                    split_high(n + AHEAD)
                for g, (piece, *_) in enumerate(GROUPS):
                    if piece == n:
                        if q and g == GROUPS_BEFORE_QUAD[q]:
                            copy_sums(q - 1)
                        if g == DENSE_FROM + 1:
                            dense_high_parts()
                        for kind, x in TILES_AFTER.get(g, []):
                            if kind == "moving" and x in LATE_FIELDS:
                                high_part(x)
                            copy_tile((kind, x))
                        for f in fields_after(g):
                            if f not in LATE_FIELDS:
                                high_part(f)
            copy_sums(QUADS - 1)

            act.wait_ge(small_loaded, 16 * len(small_loads))
            act.wait_ge(z_ready, 1)
            nc.scalar.activation(z_sb[:, 0, :], z_ps[:, 0, :], ACT.Identity, bias=b_sb[:, 0:1]).then_inc(z_copied, 1)
            for n in (0, 2):
                act.wait_ge(h1_ready, n + 1)
                nc.scalar.activation(h1_sb[:, n, :], h1_ps[:, n, :], ACT.Relu,
                                     bias=b1_sb[:, n:n + 1]).then_inc(h1_even, 1)
            act.wait_ge(h2_ready, 1)
            nc.scalar.activation(h2_sb[:, 0, :], h2_ps[0], ACT.Relu, bias=b2_sb[:, 0:1]).then_inc(h2_even, 1)
            act.wait_ge(y_ready, 1)
            nc.scalar.copy(y_sb, y_ps).then_inc(y_copied, 1)

        @block.vector
        def _(dve):
            def split_low(n):
                q, r = PIECES[n]
                dve.wait_ge(k_high_ready, n + 1)
                for row, c, _, _ in loads_of(q, r):
                    raw, high, low = k_views(n, row, c)
                    last = nc.vector.tensor_tensor(low, raw, high, ALU.subtract)
                last.then_inc(k_split_dve, 1)

            def low_part(f):
                dve.wait_ge(high_ready, GATHERED.index(f) + 1)
                high = parts[:, f % (2 * QUAD), :, 0, :]
                nc.vector.tensor_tensor(parts[:, f % (2 * QUAD), :, 1, :], nat_of(f), high,
                                        ALU.subtract).then_inc(parts_ready, 1)

            def add_sums(q):
                dve.wait_ge(pij_copied, q + 1)
                nc.vector.tensor_tensor(pij[:, CHUNK[q], :], late_sums[:], pij[:, CHUNK[q], :],
                                        ALU.add).then_inc(pij_added, 1)

            def multiply(g, half):
                _, q, r, batches = GROUPS[g]
                kind, units = batches[half]
                n = 2 * g + half
                k = units[0][0]
                dve.wait_ge(t_ready, n + 1)
                if half == 0 or kind == SINGLE:
                    dve.wait_ge(tile_copied, TILE["factor", k + (kind == SINGLE)] + 1)
                if kind == FULL:
                    if n >= PRODUCTS:
                        dve.wait_ge(reduced, (n - PRODUCTS) // 2 + 1)
                    nc.vector.tensor_tensor(prod[:, n % PRODUCTS, :, :], t_ps[:, n % T_BUFS, :, :],
                                            factor[:, k:k + 1, :].broadcast_to([P, 2, BATCH]),
                                            ALU.mult).then_inc(multiplied, 1)
                else:
                    if q:
                        dve.wait_ge(reduced, GROUPS_BEFORE_QUAD[q])
                    nc.vector.tensor_tensor(prod1[0:DIM, :, :], t_ps[0:DIM, n % T_BUFS, :, :],
                                            factor[0:DIM, k:k + 2, :], ALU.mult).then_inc(multiplied, 1)

            dve.wait_ge(ids_loaded, 16)
            nc.vector.tensor_copy(ids_f[:], ids_sb[:]).then_inc(ids_converted, 1)
            dve.wait_ge(ident_ready, 1)
            for n, f in enumerate(PICKED):
                last = nc.vector.tensor_copy(row_pick[:, n, :], ident[0:FIELDS, f:f + 1].broadcast_to([FIELDS, P]))
            last.then_inc(constants_ready, 1)
            dve.wait_ge(numbered, 1)
            nc.vector.tensor_copy(first_row[:], first_row_i[:]).then_inc(first_row_ready, 1)
            dve.wait_ge(first_row_ready, 1)
            nc.vector.memset(add_halves[:].bitcast(F32), 0.0)
            nc.vector.memset(select[:], 0.0).then_inc(zeroed_dve, 1)
            dve.wait_ge(zeroed_dve, 1)
            for h in range(2):
                side = slice(DIM * h, DIM * h + DIM)
                last = nc.vector.tensor_copy(add_halves[side, DIM:2 * DIM], ident[side, side])
            last.then_inc(constants_ready, 1)
            nc.vector.memset(select[0:DIM, 30:31], 1.0)
            nc.vector.memset(select[DIM:P, 31:32], 1.0)
            nc.vector.memset(pij[0:32, CHUNK[0], :], 0.0)
            nc.vector.memset(prod1[DIM:P, :, :], 0.0)

            def dense_low_parts():
                dve.wait_ge(dense_high, 1)
                for part in (1, 3):
                    nc.vector.tensor_tensor(dense_parts[:, :, part, 0:DENSE], dense_sb[:],
                                            dense_parts[:, :, 0, 0:DENSE], ALU.subtract)
                for part in (2, 3):
                    rows = slice(32 * part, 32 * part + DENSE)
                    last = nc.vector.tensor_tensor(w1d_parts[rows, :], w1d_sb[rows, :], w1d_parts[rows, :],
                                                   ALU.subtract)
                last.then_inc(dense_split, 1)

            def make_one_hots(n):
                f = PICKED[n]
                rows = rows_of[f]
                dve.wait_ge(table_high_ready, n + 1)
                nc.vector.tensor_tensor(table_parts[0:rows, n % 2, 0:cuts[f], 1, :], table_raw[0:rows, n, 0:cuts[f], :],
                                        table_parts[0:rows, n % 2, 0:cuts[f], 0, :],
                                        ALU.subtract).then_inc(table_split, 1)
                dve.wait_ge(tile_copied, TILE["index", f] + 1)
                for c in range(cuts[f]):
                    made = sum(cuts[x] for x in PICKED[:n]) + c
                    if made >= ONE_HOTS:
                        wait_used(dve, made - ONE_HOTS)
                    nc.vector.tensor_scalar(one_hot[made % ONE_HOTS][0:rows, :], index[0:rows, n, :], float(c),
                                            first_row[0:rows, n:n + 1], ALU.subtract, ALU.is_equal).then_inc(one_hot_ready, 1)

            make_one_hots(0)
            low_part(0)
            make_one_hots(1)
            low_part(1)
            low_part(2)
            split_low(0)
            make_one_hots(2)
            split_low(1)
            low_part(4)
            low_part(5)
            multiply(0, 0)
            multiply(0, 1)
            g = 0
            for n, (q, r) in enumerate(PIECES):
                for nth in range(len(groups_of(q, r))):
                    if g:
                        multiply(g, 0)
                        multiply(g, 1)
                    for f in fields_after(g):
                        low_part(f)
                    if g == DENSE_FROM:
                        nc.vector.memset(dense_parts.bitcast(F32), 0.0)
                        nc.vector.memset(w1d_parts.bitcast(F32), 0.0).then_inc(dense_zeroed, 1)
                    if g == DENSE_FROM + 2:
                        dense_low_parts()
                    if nth == 0 and n + AHEAD in DVE_PIECES:
                        split_low(n + AHEAD)
                    if q and g - 3 == GROUPS_BEFORE_QUAD[q] and q - 1 in ADDED:
                        add_sums(q - 1)
                    g += 1

            dve.wait_ge(small_loaded, 16 * len(small_loads))
            dve.wait_ge(z_ready, 2)
            nc.vector.tensor_scalar(z_sb[:, 1, :], z_ps[:, 1, :], b_sb[:, 1:2], None, ALU.add).then_inc(z_copied_dve, 1)
            for n in (1, 3):
                dve.wait_ge(h1_ready, n + 1)
                nc.vector.tensor_scalar(h1_sb[:, n, :], h1_ps[:, n, :], b1_sb[:, n:n + 1], 0.0,
                                        ALU.add, ALU.max).then_inc(h1_odd, 1)
            dve.wait_ge(h2_ready, 2)
            nc.vector.tensor_scalar(h2_sb[:, 1, :], h2_ps[1], b2_sb[:, 1:2], 0.0,
                                    ALU.add, ALU.max).then_inc(h2_odd, 1)

        @block.tensor
        def _(pe):
            def free_tile(n):
                earlier = [m for m in range(n) if in_t_ps(m) == in_t_ps(n)]
                if earlier:
                    pe.wait_ge(tile_copied, earlier[-1] + 1)

            def make_tile(tile):
                kind, x = tile
                n = TILE[tile]
                free_tile(n)
                if kind == "ids":
                    pe.wait_ge(ids_converted, 1)
                elif kind == "moving":
                    pe.wait_ge(parts_ready, GATHERED.index(x) + 1)
                elif kind == "w":
                    pe.wait_ge(slots_ready, 1)
                elif kind == "dense":
                    pe.wait_ge(dense_split, 1)
                for s in range(4):
                    rows = P
                    if kind == "w":
                        chunk, c = (4 * x + s) // 2, s % 2
                        if chunk == CHUNKS:
                            break
                        of = w_slots[:, c, chunk, :, :].rearrange("p k i -> p (k i)")
                    elif kind == "dense":
                        of = dense_parts[:, s, :, :].bitcast(F32).rearrange("p s n -> p (s n)")
                    elif kind == "ids":
                        of, rows = ids_f[:, s, :], FIELDS
                    elif kind == "moving":
                        of = parts[:, x % (2 * QUAD), s, :, :].bitcast(F32).rearrange("p h e -> p (h e)")
                    else:
                        of = nat[:, x % (2 * NAT_QUADS), s, :, :].rearrange("p h e -> p (h e)")
                    last = nc.tensor.transpose(tile_bank(n)[0:rows, P * s:P * s + P], of, ident[:])
                last.then_inc(transposed, 1)

            def make_index(f):
                n = TILE["index", f]
                pe.wait_ge(constants_ready, 1)
                pe.wait_ge(tile_copied, 1)
                free_tile(n)
                nc.tensor.matmul(tile_bank(n), row_pick[:, PICKED.index(f), :], ids_t[:], start=True,
                                 stop=True).then_inc(transposed, 1)

            def pick(f):
                n = PICKED.index(f)
                made = sum(cuts[x] for x in PICKED[:n])
                pe.wait_ge(table_split, n + 1)
                free_tile(TILE["moving", f])
                for c in range(cuts[f]):
                    pe.wait_ge(one_hot_ready, made + c + 1)
                    one = nc.tensor.matmul(
                        tile_bank(TILE["moving", f]), table_parts[0:rows_of[f], n % 2, c, :, :].rearrange("p h e -> p (h e)"),
                        one_hot[(made + c) % ONE_HOTS][0:rows_of[f], :],
                        start=c == 0, stop=c == cuts[f] - 1)
                    one.then_inc(one_hot_used if c < cuts[f] - 1 else transposed, 1)

            def add_parts(k):
                n = TILE["factor", k]
                pe.wait_ge(constants_ready, 2)
                free_tile(n)
                pe.wait_ge(tile_copied, max([0] + [TILE["moving", f] + 1 for f in (2 * k, 2 * k + 1)]))
                for h in range(2):
                    f = 2 * k + h
                    last = nc.tensor.matmul(tile_bank(n), add_halves[:, DIM * (1 - h):DIM * (1 - h) + P],
                                            moving[:, f // QUAD % 2, f % QUAD, :], start=h == 0, stop=h == 1)
                last.then_inc(transposed, 1)

            def make(tile):
                if tile[0] == "factor" and {2 * tile[1], 2 * tile[1] + 1} & set(PICKED):
                    add_parts(tile[1])
                elif tile[0] == "moving" and tile[1] in PICKED:
                    pick(tile[1])
                else:
                    make_tile(tile)

            def contract(g):
                n, q, r, batches = GROUPS[g]
                first_of_piece = g == 0 or GROUPS[g - 1][0] != n
                if first_of_piece:
                    wait_split(pe, n)
                    pe.wait_ge(tile_copied, FIELDS_DONE[q])
                for half, (_, units) in enumerate(batches):
                    batch = 2 * g + half
                    if batch >= T_BUFS:
                        pe.wait_ge(multiplied, batch - T_BUFS + 1)
                    for u, (k, c) in enumerate(units):
                        for which, part in enumerate((k_high, k_low)):
                            last = nc.tensor.matmul(t_ps[:, batch % T_BUFS, u, :],
                                                    part[:, n % SPLIT, k - 2 * r, c, :],
                                                    moving[:, q % 2, c, :],
                                                    start=which == 0, stop=which == 1)
                    last.then_inc(t_ready, 1)

            def reduce(g):
                _, q, r, batches = GROUPS[g]
                if g == GROUPS_BEFORE_QUAD[q] and q:
                    pe.wait_ge(pij_copied, q)
                pe.wait_ge(multiplied, 2 * g + 2)
                for half, (kind, units) in enumerate(batches):
                    for u, (k, c) in enumerate(units):
                        of = prod[:, (2 * g + half) % PRODUCTS, u, :] if kind == FULL else prod1[:, u, :]
                        last = nc.tensor.matmul(sum_ps[32 * c:32 * c + 32, :],
                                                select[:, 30 - 2 * k - FIRST_ROW[q]:62 - 2 * k - FIRST_ROW[q]], of,
                                                start=k == 0, stop=k == LAST_UNIT[q, c])
                last.then_inc(reduced, 1)

            pe.wait_ge(ident_ready, 1)
            make(("ids", 0))
            for f in PICKED:
                make_index(f)
            for tile in FIRST_TILES[1 + len(PICKED):]:
                make(tile)
            for g in range(len(GROUPS)):
                contract(g)
                if g:
                    reduce(g - 1)
                for tile in TILES_AFTER.get(g, []):
                    make(tile)

            def add_z(c, chunk, start, stop):
                at = chunk * Z_OUT + P * c
                return nc.tensor.matmul(z_ps[:, c, :], w_t[:, at:at + P], pij[:, chunk, :], start=start, stop=stop)

            pe.wait_ge(multiplied, 2 * len(GROUPS) - 2)
            wait_sums(pe, 3)
            wait_sums(pe, 6)
            early = [chunk for chunk in range(CHUNKS) if chunk != CHUNK[QUADS - 1]]
            for c in range(2):
                for chunk in early:
                    add_z(c, chunk, chunk == early[0], False)
            reduce(len(GROUPS) - 1)
            pe.wait_ge(multiplied, 2 * len(GROUPS))
            pe.wait_ge(tile_copied, len(TILES))
            for n in range(4):
                nc.tensor.matmul(h1_ps[:, n, :], w1d_parts[:, n::4], dense_t, start=True, stop=False)
            wait_sums(pe, QUADS - 1)
            for c in range(2):
                add_z(c, CHUNK[QUADS - 1], False, True).then_inc(z_ready, 1)
            for c in range(2):
                pe.wait_ge((z_copied, z_copied_dve)[c], 1)
                for n in range(4):
                    last = nc.tensor.matmul(h1_ps[:, n, :], w1_sb[:, c, n::4], z_sb[:, c, :],
                                            start=False, stop=c == 1)
                    if c == 1:
                        last.then_inc(h1_ready, 1)
            for c in range(4):
                pe.wait_ge(h1_odd if c % 2 else h1_even, c // 2 + 1)
                for n in range(2):
                    last = nc.tensor.matmul(h2_ps[n], w2_sb[:, c, n::2], h1_sb[:, c, :],
                                            start=c == 0, stop=c == 3)
                    if c == 3:
                        last.then_inc(h2_ready, 1)
            for c in range(2):
                pe.wait_ge(h2_odd if c else h2_even, 1)
                last = nc.tensor.matmul(y_ps, w3_sb[:, c:c + 1], h2_sb[:, c, :], start=c == 0, stop=c == 1)
            last.then_inc(y_ready, 1)


_TABLES = [f"tbl_{f}" for f in range(FIELDS)]
_INS = ["dense_ctx", "ids"] + _TABLES + ["W_top1", "b_top1", "W_top2", "b_top2", "W_top3",
                                          "L0_rec_kernel", "L0_rec_W", "L0_rec_b"]


def kernel(**inputs):
    import numpy as _np
    import concourse.bacc as _bacc
    from concourse import mybir as _mybir
    from concourse.bass_utils import run_bass_kernel_spmd as _run

    nc = _bacc.Bacc("TRN2", target_bir_lowering=False, num_devices=1)
    arrays, args = {}, {}
    for name in _INS:
        a = _np.ascontiguousarray(inputs[name])
        arrays[f"in_{name}"] = a
        args[name] = nc.dram_tensor(f"in_{name}", a.shape, _mybir.dt.from_np(a.dtype), kind="ExternalInput").ap()
    out = nc.dram_tensor("out_y", (BATCH, 1), _mybir.dt.float32, kind="ExternalOutput").ap()
    build(nc, args["dense_ctx"], args["ids"], [args[t] for t in _TABLES], args["W_top1"], args["b_top1"],
          args["W_top2"], args["b_top2"], args["W_top3"], args["L0_rec_kernel"], args["L0_rec_W"],
          args["L0_rec_b"], out)
    r = _run(nc, [arrays], core_ids=[0])
    return r.results[0]["out_y"]
```
